# Optimizing a Trainium2 kernel written in Bass

```python
import numpy as np
import jax
import jax.numpy as jnp

def _softmax(x, axis=-1):
    return jax.nn.softmax(x, axis=axis)

def _gelu(x):
    return jax.nn.gelu(x, approximate=True)

def _silu(x):
    return jax.nn.silu(x)

def _sigmoid(x):
    return jax.nn.sigmoid(x)

def _layernorm(x, axis=-1, eps=1e-05):
    m = jnp.mean(x, axis=axis, keepdims=True)
    v = jnp.var(x, axis=axis, keepdims=True)
    return (x - m) / jnp.sqrt(v + eps)

def _scatter_add(tgt, idx, src, axis=0):
    return tgt.at[idx].add(src)

def _segment_sum(src, seg, n):
    return jax.ops.segment_sum(src, seg, n)
kernel_name = 'mk_adj_resnorm_d1_adj_r2_0d219b'

def setup_inputs(seed: int=0):
    np.random.seed(seed)
    _w = jnp.asarray

    def _rec_inputs():
        import jax
        import jax.numpy as jnp
        _gk = jax.random.key(seed)
        x = -0.000929 + 1 * jax.random.normal(jax.random.fold_in(_gk, 1), (8, 2048, 64), jnp.float32)
        _a = jax.random.bernoulli(jax.random.fold_in(_gk, 2), 0.0078125, (8, 2048, 2048))
        _a = jnp.logical_or(_a, jnp.swapaxes(_a, -1, -2))
        _a = jnp.logical_or(_a, jnp.eye(2048, dtype=bool))
        _af = _a.astype(jnp.float32)
        _af = _af * jax.random.uniform(jax.random.fold_in(_gk, 3), (8, 2048, 2048), jnp.float32, 0.05, 1)
        adj = _af
        return (x, adj)
    x, adj = _rec_inputs()

    def _L0_gnn_setup():
        import jax, jax.numpy as jnp
        import numpy as np
        B, N, C, R = (4, 2048, 64, 16)
        EPS = 1e-12
        key = jax.random.key(seed)
        k_x, k_w, k_u = jax.random.split(key, 3)
        x = jax.random.normal(k_x, (B, N, C), dtype=jnp.float32)
        W = jax.random.uniform(k_w, (B, N, N), dtype=jnp.float32)
        U = 0.01 * jax.random.normal(k_u, (N, R), dtype=jnp.float32)
        w_scale = jnp.asarray(1.0, dtype=jnp.float32)
        return {'x': x, 'W': W, 'U': U, 'w_scale': w_scale}
    _L0_gnn_all = _L0_gnn_setup()
    _L0_gnn_in = {k: v for k, v in _L0_gnn_all.items() if k in ('U', 'w_scale')}
    del _L0_gnn_all
    return {'x': x, 'adj': adj, 'L0_gnn_U': _L0_gnn_in['U'], 'L0_gnn_w_scale': _L0_gnn_in['w_scale']}

def reference(x, adj, L0_gnn_U, L0_gnn_w_scale):
    import jax
    import jax.numpy as jnp

    def _L0_gnn_ref(x, W, U, w_scale):
        import jax, jax.numpy as jnp
        import numpy as np
        B, N, C, R = (4, 2048, 64, 16)
        EPS = 1e-12
        Ws = 0.5 * (W + jnp.swapaxes(W, -1, -2))
        A = jax.nn.sigmoid(U @ U.T)
        K = Ws * A[None, :, :]
        deg = jnp.maximum(K.sum(axis=-1), EPS)
        d = jax.lax.rsqrt(deg)
        K = K * d[:, :, None] * d[:, None, :]
        return w_scale * jnp.einsum('bnm,bmc->bnc', K, x)
    x = _layernorm(x + _L0_gnn_ref(x, adj, L0_gnn_U, L0_gnn_w_scale), axis=-1)
    return x

_drawn_inputs = setup_inputs


def setup_inputs(seed=0):
    import zlib

    import numpy as np

    out = dict(_drawn_inputs(seed))
    spreads = {}
    factors = {'L0_gnn_U': 64.0}
    for name, (base, spread) in spreads.items():
        noise = np.random.default_rng([zlib.crc32(name.encode()), seed]).standard_normal(out[name].shape)
        drawn = base * np.exp(spread * noise) if base else spread * noise
        out[name] = jnp.asarray(drawn.astype(out[name].dtype))
    for name, factor in factors.items():
        out[name] = (out[name] * factor).astype(out[name].dtype)
    return out
```

```python
from contextlib import ExitStack

import concourse.bass as bass
from concourse import mybir

F32 = mybir.dt.float32
ALU = mybir.AluOpType
ACT = mybir.ActivationFunctionType
AX = mybir.AxisListType

B, N, C, R = 8, 2048, 64, 16
P = 128
SB = 512
KB = SB // P
NT = N // P
DEG_EPS = 1e-12
LN_EPS = 1e-5

UNITS = [(0, 1), (2, 3), (0, 3), (1, 2), (0, 0), (1, 1), (2, 2), (3, 3), (0, 2), (1, 3)]
DOUBLED = 2
SUPERUNITS = [[(0, 3)], [(1, 2)], [(0, 0), (1, 1)], [(2, 2), (3, 3)], [(0, 2), (1, 3)], [(0, 1)], [(2, 3)]]

W_SLOTS = 4
MIRROR_BANKS = 4
BACK_BANKS = 2
BACK_SLOTS = 4


def first_block(I, J, k):
    return k if I == J else 0


CHUNKS = [(u, I, J, k, P * first_block(I, J, k), SB - P * first_block(I, J, k))
          for u, (I, J) in enumerate(UNITS) for k in range(KB)]
NC = len(CHUNKS)


def places():
    a_at, s_at, at, end = {}, {}, 0, 0
    for u, I, J, k, _, width in CHUNKS:
        a_at[I, J, k] = at
        at += width
        for parity in range(2):
            if parity == 1 and u >= DOUBLED:
                s_at[1, I, J, k] = s_at[0, I, J, k]
            else:
                s_at[parity, I, J, k] = end
                end += width
    return a_at, s_at, at, end


A_AT, S_AT, A_COLS, S_COLS = places()


def loads():
    out = []
    for u, (I, J) in enumerate(UNITS):
        if I != J:
            out.append((J, I, u, True))
        out.append((I, J, u, False))
    return out


LOADS = loads()
NL = len(LOADS)
LOAD_OF = {(row, col): m for m, (row, col, _, _) in enumerate(LOADS)}
assert NL % W_SLOTS == 0 and NC % MIRROR_BANKS == 0

FIRST_UNIT = {J: next((I, K) for I, K in UNITS if K == J) for J in range(N // SB)}
NCOL = sum(not (I == J and k == KB - 1) and not (k == 0 and FIRST_UNIT[J] == (I, J))
           for _, I, J, k, _, _ in CHUNKS) + sum(I == J for J, (I, _) in FIRST_UNIT.items())


def groups():
    out, n, ends = [], 0, {}
    for superunit in SUPERUNITS:
        for k in range(KB):
            natural, back = [], []
            for I, J in superunit:
                natural.append((I, J, k))
                blocks = k if I == J else KB
                if blocks:
                    back.append((I, J, k, blocks, n))
                    n += 1
            out.append((natural, back))
        for unit in superunit:
            ends[unit] = n
    return out, n, ends


GROUPS, NB, UNIT_DONE = groups()
assert NB % BACK_BANKS == 0 and NB % BACK_SLOTS == 0


def ends_of_sums():
    first, last = {}, {}
    for g, (natural, back_products) in enumerate(GROUPS):
        for kind, targets in (("natural", [J for _, J, _ in natural]), ("back", [b[0] for b in back_products])):
            for J in targets:
                first.setdefault(J, (g, kind))
                last[J] = (g, kind)
    return first, last


FIRST, LAST = ends_of_sums()

RESIDUAL_AT, DEGREES_AT, SCALE_AT, VARIANCE_AT, SHIFTS_AT = (1, 4), 2, 3, 26, 28
TURN_Y_AT, SUM_AT = 1, 3
X_LOAD_AT = LOAD_OF[0, 0]
SQUARES_AT, ROOT_AT = 2, 26


def tensor_order(mirrors, products):
    order, c, g, t_mirror, t_group = [], 0, 0, 0.0, 6.1
    while c < (NC if mirrors else 0) or g < (len(GROUPS) if products else 0):
        if g >= len(GROUPS) or not products or (mirrors and c < NC and t_mirror <= t_group):
            order.append(("mirror", c))
            t_mirror += 0.134 + CHUNKS[c][5] * 2.08e-3 + (3.0 if c == 5 else 0.0)
            c += 1
        else:
            order.append(("group", g))
            natural, back = GROUPS[g]
            t_group += sum(1.15 for _ in back) if natural[0][0] != natural[0][1] else 1.3
            g += 1
    return order


def propagate(nc, x, adj, U, w_scale, out):
    with ExitStack() as ctx:
        def sbuf(name, shape):
            return ctx.enter_context(nc.sbuf_tensor(name, shape, F32))

        def psum(name, shape):
            return ctx.enter_context(nc.psum_tensor(name, shape, F32))

        def sem(name):
            return ctx.enter_context(nc.semaphore(name))

        a_store = sbuf("a_store", [P, A_COLS])
        s_store = sbuf("s_store", [P, S_COLS])
        w_ring = sbuf("w_ring", [P, W_SLOTS, KB, SB])
        back = sbuf("back", [P, BACK_SLOTS, SB])
        colacc = sbuf("colacc", [P, N])
        x_in = [sbuf(f"x_in{i}", [P, NT, C]) for i in range(2)]
        x_scaled = sbuf("x_scaled", [P, NT, C])
        y_t = sbuf("y_t", [P, 2, SB])
        res = sbuf("res", [P, NT, C])
        ident = sbuf("ident", [P, P])
        ones = sbuf("ones", [P, 32])
        row_sums = [sbuf(f"row_sums{i}", [P, NT, KB]) for i in range(2)]
        row_sum = sbuf("row_sum", [P, NT])
        deg = sbuf("deg", [P, NT])
        deg_half = sbuf("deg_half", [P, NT])
        deg_inv = sbuf("deg_inv", [P, NT])
        d = sbuf("d", [P, NT])
        d_half = sbuf("d_half", [P, NT])
        d_scale = [sbuf(f"d_scale{i}", [P, NT]) for i in range(2)]
        w_col = sbuf("w_col", [P, 1])
        sums = sbuf("sums", [P, NT])
        neg_mean = sbuf("neg_mean", [P, NT])
        squares = sbuf("squares", [P, NT])
        var = sbuf("var", [P, NT])
        var_inv = sbuf("var_inv", [P, NT])
        rstd = sbuf("rstd", [P, NT])
        shift = sbuf("shift", [P, NT])
        u_in = res[:, :, :].rearrange("p t c -> p (t c)")[:, 0:NT * R]
        u_t = back[0:R, :, :].rearrange("p s c -> p (s c)")
        col_sums = back[:, 0, :]

        y = psum("y", [P, 2, SB])
        mirror = psum("mirror", [P, MIRROR_BANKS, SB])
        turned = psum("turned", [P, BACK_BANKS, SB])

        w_landed = [sem(f"w_landed{i}") for i in range(W_SLOTS)]
        x_landed = [sem(f"x_landed{i}") for i in range(2)]
        u_landed = sem("u_landed")
        scale_landed = sem("scale_landed")
        out_stored = sem("out_stored")
        consts_ready = sem("consts_ready")
        ident_zero = sem("ident_zero")
        rows_clear = sem("rows_clear")
        u_turned = sem("u_turned")
        u_t_ready = sem("u_t_ready")
        a_logits = sem("a_logits")
        a_ready = sem("a_ready")
        mirrored = sem("mirrored")
        summed = sem("summed")
        s_ready = sem("s_ready")
        cols_added = sem("cols_added")
        col_summed = sem("col_summed")
        col_copied = sem("col_copied")
        deg_turned = sem("deg_turned")
        row_summed = sem("row_summed")
        deg_added = sem("deg_added")
        deg_bounded = sem("deg_bounded")
        d_halved = sem("d_halved")
        d_scaled = sem("d_scaled")
        inv_ready = sem("inv_ready")
        d_ready = sem("d_ready")
        x_ready = sem("x_ready")
        s_turned = sem("s_turned")
        back_ready = sem("back_ready")
        back_used = sem("back_used")
        y_copied = sem("y_copied")
        y_turned = sem("y_turned")
        res_ready = sem("res_ready")
        mean_ready = sem("mean_ready")
        squared = sem("squared")
        var_added = sem("var_added")
        var_ready = sem("var_ready")
        rstd_ready = sem("rstd_ready")
        shift_ready = sem("shift_ready")
        normed = sem("normed")

        block = ctx.enter_context(nc.Block())

        def due(count):
            return not isinstance(count, int) or count > 0

        def col_part(parity, c):
            _, I, J, k, col0, width = CHUNKS[c]
            skip = P if I == J else 0
            if width == skip:
                return None
            at = S_AT[parity, I, J, k]
            return (col0 + skip, width - skip), s_store[:, at + skip:at + width]

        def x_count(p, parity):
            return (p - parity) * 8 + 16

        def lane(J):
            return slice(C * (J % 2), C * (J % 2) + C)

        def all_steps(eng, step):
            step(0, 0)
            step(1, 1)
            with eng.Fori(2, B - 1, 2) as b:
                step(b, 0)
                step(b + 1, 1)
            step(B, B % 2)
            step(B + 1, (B + 1) % 2)

        def has(b, lag):
            return not isinstance(b, int) or 0 <= b - lag < B

        @block.sync
        def _(sp):
            def step(b, parity):
                if not has(b, 0):
                    return
                for m, (row, col, u, _) in enumerate(LOADS):
                    before = (m - W_SLOTS) % NL
                    batch_before = b if m >= W_SLOTS else b - 1
                    if has(batch_before, 0):
                        last_chunk = KB * LOADS[before][2] + KB
                        if LOADS[before][3]:
                            sp.wait_ge(mirrored, batch_before * NC + last_chunk)
                        else:
                            sp.wait_ge(summed, batch_before * NC + last_chunk)
                    if m == X_LOAD_AT:
                        sp.dma_start(x_in[parity][:, :, :],
                                     x[bass.ds(b, 1), :, :].rearrange("o (t p) c -> p (o t) c", p=P))\
                            .then_inc(x_landed[parity], 16)
                    sp.dma_start(w_ring[:, m % W_SLOTS, :, :],
                                 adj[bass.ds(b, 1), row * SB:(row + 1) * SB, col * SB:(col + 1) * SB]
                                 .rearrange("o (k p) c -> p (o k) c", p=P)).then_inc(w_landed[m % W_SLOTS], 16)

            all_steps(sp, step)
            sp.wait_ge(out_stored, 16 * B)

        @block.gpsimd
        def _(pool):
            pool.memset(ident[:, :], 0.0).then_inc(ident_zero, 1)
            pool.memset(ones[:, :], 1.0).then_inc(consts_ready, 1)
            pool.wait_ge(ident_zero, 1)
            pool.affine_select(out=ident[:, :], in_=ident[:, :], compare_op=ALU.not_equal, fill=1.0, base=0,
                               pattern=[[-1, P]], channel_multiplier=1).then_inc(consts_ready, 1)

            pool.memset(colacc[:, 0:P], 0.0).then_inc(consts_ready, 1)

            def step(b, parity):
                if not has(b, 0):
                    return
                if due(count := b):
                    pool.wait_ge(col_summed, count)
                done = 0
                for c, (_, I, J, k, _, _) in enumerate(CHUNKS):
                    part = col_part(parity, c)
                    if part is None or (k == 0 and FIRST_UNIT[J] == (I, J)):
                        continue
                    (first, width), chunk = part
                    acc = colacc[:, J * SB + first:J * SB + SB]
                    pool.wait_ge(s_ready, b * NC + c + 1)
                    if k == 1 and FIRST_UNIT[J] == (I, J):
                        (first0, width0), chunk0 = col_part(parity, c - 1)
                        pool.tensor_tensor(acc, chunk0[:, width0 - width:width0], chunk, ALU.add)\
                            .then_inc(cols_added, 1)
                        if first0 < first:
                            pool.tensor_copy(colacc[:, J * SB + first0:J * SB + first], chunk0[:, 0:width0 - width])\
                                .then_inc(cols_added, 1)
                            done += 1
                    else:
                        if due(count := b * NCOL + done):
                            pool.wait_ge(cols_added, count)
                        pool.tensor_tensor(acc, acc, chunk, ALU.add).then_inc(cols_added, 1)
                    done += 1
                assert done == NCOL

            all_steps(pool, step)

        @block.vector
        def _(dve):
            for i in range(2):
                dve.memset(row_sums[i][:, :, :], 0.0).then_inc(rows_clear, 1)
            dve.wait_ge(rows_clear, 2)
            dve.wait_ge(scale_landed, 16)

            def add_mirror(b, c):
                _, I, J, k, col0, width = CHUNKS[c]
                m = LOAD_OF[I, J]
                dve.wait_ge(mirrored, b * NC + c + 1)
                if k == 0:
                    dve.wait_ge(w_landed[m % W_SLOTS], 16 * (b * (NL // W_SLOTS) + m // W_SLOTS + 1))
                bank = mirror[:, c % MIRROR_BANKS, 0:width]
                dve.tensor_tensor(bank, bank, w_ring[:, m % W_SLOTS, k, col0:SB], ALU.add).then_inc(summed, 1)

            def times_a(b, parity, c):
                u, I, J, k, col0, width = CHUNKS[c]
                dve.wait_ge(summed, b * NC + c + 1)
                if isinstance(b, int) and b == 0:
                    dve.wait_ge(a_ready, c + 1)
                if k == 0:
                    if u >= DOUBLED:
                        if due(count := (b - 1) * NB + UNIT_DONE[I, J]):
                            dve.wait_ge(back_used, count)
                    elif u == 0:
                        if due(count := (b - 1) * NB):
                            dve.wait_ge(back_used, count)
                at, a0 = S_AT[parity, I, J, k], A_AT[I, J, k]
                dve.scalar_tensor_tensor(out=s_store[:, at:at + width], in0=mirror[:, c % MIRROR_BANKS, 0:width],
                                         scalar=1.0, in1=a_store[:, a0:a0 + width], op0=ALU.mult, op1=ALU.mult,
                                         accum_out=row_sums[parity][:, KB * I + k, J:J + 1]).then_inc(s_ready, 1)

            def degrees(p, parity):
                dve.wait_ge(s_ready, (p + 1) * NC)
                dve.tensor_reduce(out=row_sum[:, :], in_=row_sums[parity][:, :, :], axis=AX.X, op=ALU.add)\
                    .then_inc(row_summed, 1)
                dve.wait_ge(row_summed, p + 1)
                dve.wait_ge(deg_turned, p + 1)
                by_node = turned[:, 1, :].rearrange("p (k j q) -> p j k q", k=KB, j=KB)[:, :, :, 0]
                dve.tensor_tensor(deg[:, :].rearrange("p (j k) -> p j k", j=KB), by_node,
                                  row_sum[:, :].rearrange("p (j k) -> p j k", j=KB), ALU.add).then_inc(deg_added, 1)
                dve.wait_ge(deg_added, p + 1)
                dve.tensor_scalar(deg_half[:, :], deg[:, :], 0.5, DEG_EPS, ALU.mult, ALU.max).then_inc(deg_bounded, 1)
                dve.wait_ge(deg_bounded, p + 1)
                dve.reciprocal(deg_inv[:, :], deg_half[:, :]).then_inc(inv_ready, 1)

            def scale_x(p, parity):
                dve.wait_ge(d_ready, p + 1)
                dve.tensor_scalar(d_half[:, :], d[:, :], 0.5, None, ALU.mult).then_inc(d_halved, 1)
                dve.tensor_scalar(d_scale[parity][:, :], d[:, :], w_col[:, 0:1], None, ALU.mult).then_inc(d_scaled, 1)
                dve.wait_ge(d_halved, p + 1)
                dve.wait_ge(x_landed[parity], x_count(p, parity))
                if due(count := p * NB):
                    dve.wait_ge(back_used, count)
                dve.tensor_tensor(x_scaled[:, :, :], x_in[parity][:, :, :],
                                  d_half[:, :].rearrange("p (t o) -> p t o", o=1).broadcast_to([P, NT, C]), ALU.mult)\
                    .then_inc(x_ready, 1)

            def residual(q, parity, bank):
                dve.wait_ge(y_turned, 2 * q + bank + 1)
                if bank == 0:
                    if due(count := 16 * q):
                        dve.wait_ge(out_stored, count)
                    dve.wait_ge(d_scaled, q + 1)
                for lane_ in range(2):
                    for k in range(KB):
                        t = 2 * KB * bank + KB * lane_ + k
                        last = dve.scalar_tensor_tensor(
                            out=res[:, t, :], in0=y[:, bank, P * k + C * lane_:P * k + C * lane_ + C],
                            scalar=d_scale[parity][:, t:t + 1], in1=x_in[parity][:, t, :],
                            op0=ALU.mult, op1=ALU.add, accum_out=sums[:, t:t + 1])
                last.then_inc(res_ready, 1)

            def mean(q):
                dve.wait_ge(res_ready, 2 * q + 2)
                dve.tensor_scalar(neg_mean[:, :], sums[:, :], -1.0 / C, None, ALU.mult).then_inc(mean_ready, 1)

            def variance(q):
                dve.wait_ge(squared, (q + 1) * NT)
                dve.tensor_scalar(var[:, :], squares[:, :], 1.0 / C, LN_EPS, ALU.mult, ALU.add).then_inc(var_added, 1)
                dve.wait_ge(var_added, q + 1)
                dve.reciprocal(var_inv[:, :], var[:, :]).then_inc(var_ready, 1)

            def shifts(q):
                dve.wait_ge(rstd_ready, q + 1)
                dve.tensor_tensor(shift[:, :], neg_mean[:, :], rstd[:, :], ALU.mult).then_inc(shift_ready, 1)

            def step(b, parity):
                p, q = b - 1, b - 2
                if has(b, 0):
                    add_mirror(b, 0)
                for c in range(NC):
                    if has(b, 0):
                        if c + 1 < NC:
                            add_mirror(b, c + 1)
                        times_a(b, parity, c)
                    if c == RESIDUAL_AT[0] and has(b, 2):
                        residual(q, parity, 0)
                    if c == DEGREES_AT and has(b, 1):
                        degrees(p, 1 - parity)
                    if c == RESIDUAL_AT[1] and has(b, 2):
                        residual(q, parity, 1)
                        mean(q)
                    if c == SCALE_AT and has(b, 1):
                        scale_x(p, 1 - parity)
                    if c == VARIANCE_AT and has(b, 2):
                        variance(q)
                    if c == SHIFTS_AT and has(b, 2):
                        shifts(q)

            all_steps(dve, step)

        @block.scalar
        def _(act):
            act.dma_start(u_in, U.rearrange("(p t) r -> p (t r)", p=P)).then_inc(u_landed, 16)
            act.dma_start(w_col[:, :], w_scale.partition_broadcast(P)).then_inc(scale_landed, 16)
            by_tile = u_t.rearrange("r (p t) -> r t p", t=NT)
            act.wait_ge(u_turned, 1)
            act.activation(by_tile[:, 0:NT // 2, :], y[0:R, :, :].rearrange("r s (t p) -> r (s t) p", p=P), ACT.Copy)\
                .then_inc(u_t_ready, 1)
            act.activation(by_tile[:, NT // 2:NT, :], turned[0:R, :, :].rearrange("r s (t p) -> r (s t) p", p=P),
                           ACT.Copy).then_inc(u_t_ready, 1)
            for c, (_, I, J, k, _, width) in enumerate(CHUNKS):
                act.wait_ge(a_logits, c + 1)
                a0 = A_AT[I, J, k]
                act.activation(a_store[:, a0:a0 + width], turned[:, c % BACK_BANKS, 0:width], ACT.Sigmoid)\
                    .then_inc(a_ready, 1)

            def copy_y(q):
                if due(count := 2 * q):
                    act.wait_ge(y_turned, count)
                if due(count := NT * q):
                    act.wait_ge(squared, count)
                act.wait_ge(back_used, (q + 1) * NB)
                for bank in range(2):
                    act.activation(y_t[:, bank, :], y[:, bank, :], ACT.Copy).then_inc(y_copied, 1)

            def copy_column_sums(p):
                act.wait_ge(col_summed, p + 1)
                act.activation(col_sums, turned[:, 0, :], ACT.Copy).then_inc(col_copied, 1)

            def root_degrees(p):
                act.wait_ge(inv_ready, p + 1)
                act.activation(d[:, :], deg_inv[:, :], ACT.Sqrt).then_inc(d_ready, 1)

            def copy_back(p, n, blocks):
                act.wait_ge(s_turned, p * NB + n + 1)
                if n == 0:
                    act.wait_ge(deg_turned, p + 1)
                if due(count := p * NB + n + 1 - BACK_SLOTS):
                    act.wait_ge(back_used, count)
                act.activation(back[:, n % BACK_SLOTS, 0:P * blocks], turned[:, n % BACK_BANKS, 0:P * blocks],
                               ACT.Copy).then_inc(back_ready, 1)

            def square(q, t):
                if t == 0:
                    act.wait_ge(mean_ready, q + 1)
                    act.wait_ge(y_turned, 2 * q + 2)
                junk = y_t[:, t // 8, C * (t % 8):C * (t % 8) + C]
                act.activation(junk, res[:, t, :], ACT.Square, bias=neg_mean[:, t:t + 1],
                               accum_out=squares[:, t:t + 1]).then_inc(squared, 1)

            def root_variance(q):
                act.wait_ge(var_ready, q + 1)
                act.activation(rstd[:, :], var_inv[:, :], ACT.Sqrt).then_inc(rstd_ready, 1)

            def normalise(q, t):
                if t == 0:
                    act.wait_ge(shift_ready, q + 1)
                act.activation(res[:, t, :], res[:, t, :], ACT.Identity, scale=rstd[:, t:t + 1],
                               bias=shift[:, t:t + 1]).then_inc(normed, 1)
                if t == NT - 1:
                    act.wait_ge(normed, (q + 1) * NT)
                    act.dma_start(out[bass.ds(q, 1), :, :].rearrange("o (t p) c -> p (o t) c", p=P), res[:, :, :])\
                        .then_inc(out_stored, 16)

            def step(b, parity):
                p, q = b - 1, b - 2
                if has(b, 2):
                    copy_y(q)
                if has(b, 1):
                    copy_column_sums(p)
                    root_degrees(p)
                for _, back_products in GROUPS:
                    for _, _, _, blocks, n in back_products:
                        if has(b, 1):
                            copy_back(p, n, blocks)
                        if has(b, 2):
                            if SQUARES_AT <= n < SQUARES_AT + NT:
                                square(q, n - SQUARES_AT)
                            if n == ROOT_AT:
                                root_variance(q)
                            if ROOT_AT < n <= ROOT_AT + NT // 2:
                                normalise(q, 2 * (n - ROOT_AT - 1))
                                normalise(q, 2 * (n - ROOT_AT - 1) + 1)

            all_steps(act, step)

        @block.tensor
        def _(pe):
            pe.wait_ge(consts_ready, 3)
            pe.wait_ge(u_landed, 16)
            for t in range(NT):
                bank = y if t < NT // 2 else turned
                last = pe.transpose(bank[0:R, t // KB % 2, P * (t % KB):P * (t % KB) + P], u_in[:, R * t:R * t + R],
                                    ident[:, :])
            last.then_inc(u_turned, 1)
            pe.wait_ge(u_t_ready, 2)

            def logits(c):
                _, I, J, k, col0, width = CHUNKS[c]
                if c >= BACK_BANKS:
                    pe.wait_ge(a_ready, c + 1 - BACK_BANKS)
                row = I * SB + k * P
                pe.matmul(turned[:, c % BACK_BANKS, 0:width], u_t[:, row:row + P],
                          u_t[:, J * SB + col0:J * SB + SB], start=True, stop=True).then_inc(a_logits, 1)

            def turn_mirror(b, c):
                _, I, J, k, col0, _ = CHUNKS[c]
                m = LOAD_OF[J, I]
                if k == 0:
                    pe.wait_ge(w_landed[m % W_SLOTS], 16 * (b * (NL // W_SLOTS) + m // W_SLOTS + 1))
                if due(count := b * NC + c + 1 - MIRROR_BANKS):
                    pe.wait_ge(s_ready, count)
                for j in range(col0 // P, KB):
                    last = pe.transpose(mirror[:, c % MIRROR_BANKS, P * j - col0:P * j - col0 + P],
                                        w_ring[:, m % W_SLOTS, j, P * k:P * k + P], ident[:, :])
                last.then_inc(mirrored, 1)

            def sum_columns(p):
                pe.wait_ge(cols_added, (p + 1) * NCOL)
                pe.wait_ge(s_ready, (p + 1) * NC)
                if due(count := p * NB):
                    pe.wait_ge(back_ready, count)
                if isinstance(p, int) and p == 0:
                    pe.wait_ge(a_ready, NC)
                for J in range(KB):
                    last = pe.matmul(turned[32 * J:32 * J + 32, 0, :], ones[:, :], colacc[:, J * SB:J * SB + SB],
                                     start=True, stop=True)
                last.then_inc(col_summed, 1)

            def turn_column_sums(p):
                pe.wait_ge(col_copied, p + 1)
                for k in range(KB):
                    last = pe.transpose(turned[:, 1, P * k:P * k + P], col_sums[:, P * k:P * k + P], ident[:, :])
                last.then_inc(deg_turned, 1)

            def turn_y(q, bank):
                pe.wait_ge(y_copied, 2 * q + bank + 1)
                for k in range(KB):
                    last = pe.transpose(y[:, bank, P * k:P * k + P], y_t[:, bank, P * k:P * k + P], ident[:, :])
                last.then_inc(y_turned, 1)

            def turn_back(p, parity, I, J, k, blocks, n):
                if due(count := p * NB + n + 1 - BACK_BANKS):
                    pe.wait_ge(back_ready, count)
                for i in range(blocks):
                    at = S_AT[parity, I, J, i] + P * (k - first_block(I, J, i))
                    last = pe.transpose(turned[:, n % BACK_BANKS, P * i:P * i + P], s_store[:, at:at + P], ident[:, :])
                last.then_inc(s_turned, 1)

            def group_turns(p, parity, g):
                for I, J, k, blocks, n in GROUPS[g][1]:
                    turn_back(p, parity, I, J, k, blocks, n)

            def group_products(p, parity, g):
                natural, back_products = GROUPS[g]
                for I, J, k in natural:
                    at, block0 = S_AT[parity, I, J, k], first_block(I, J, k)
                    pe.matmul(y[lane(J), J // 2, P * block0:SB], x_scaled[:, KB * I + k, :],
                              s_store[:, at:at + SB - P * block0], start=FIRST[J] == (g, "natural"),
                              stop=LAST[J] == (g, "natural"))
                for I, J, k, blocks, n in back_products:
                    pe.wait_ge(back_ready, p * NB + n + 1)
                    pe.matmul(y[lane(I), I // 2, 0:P * blocks], x_scaled[:, KB * J + k, :],
                              back[:, n % BACK_SLOTS, 0:P * blocks], start=FIRST[I] == (g, "back"),
                              stop=LAST[I] == (g, "back")).then_inc(back_used, 1)

            def step(b, parity):
                p, q = b - 1, b - 2
                group = 0
                if has(b, 0) and not has(b, 1):
                    logits(0)
                    logits(1)
                for kind, n in tensor_order(has(b, 0), has(b, 1)):
                    if kind == "mirror":
                        if not has(b, 1) and n + 2 < NC:
                            logits(n + 2)
                        turn_mirror(b, n)
                    if has(b, 2) and (kind, n) == (("mirror", TURN_Y_AT) if has(b, 0) else ("group", 0)):
                        turn_y(q, 0)
                        turn_y(q, 1)
                    if has(b, 1) and (kind, n) == (("mirror", SUM_AT) if has(b, 0) else ("group", 0)):
                        sum_columns(p)
                        turn_column_sums(p)
                    if kind == "group":
                        if n == 0:
                            pe.wait_ge(x_ready, p + 1)
                            if due(count := 2 * p):
                                pe.wait_ge(res_ready, count)
                            group_turns(p, 1 - parity, 0)
                        if n + 1 < len(GROUPS):
                            group_turns(p, 1 - parity, n + 1)
                        group_products(p, 1 - parity, n)
                if has(b, 2) and not has(b, 1):
                    turn_y(q, 0)
                    turn_y(q, 1)

            all_steps(pe, step)


_INS = ["x", "adj", "L0_gnn_U", "L0_gnn_w_scale"]


def kernel(**inputs):
    import numpy as _np
    import concourse.bacc as _bacc
    from concourse import mybir as _mybir
    from concourse.bass_utils import run_bass_kernel_spmd as _run

    nc = _bacc.Bacc("TRN2", target_bir_lowering=False, num_devices=1, dynamic_dma_scratch_size=1024)
    arrays, args = {}, []
    for name in _INS:
        a = _np.ascontiguousarray(inputs[name])
        if a.ndim == 0:
            a = a.reshape(1)
        arrays[f"in_{name}_dram"] = a
        args.append(nc.dram_tensor(f"in_{name}_dram", a.shape, _mybir.dt.from_np(a.dtype), kind="ExternalInput").ap())
    out = nc.dram_tensor("out_0_dram", (B, N, C), _mybir.dt.float32, kind="ExternalOutput").ap()
    propagate(nc, *args, out)
    r = _run(nc, [arrays], core_ids=[0])
    return r.results[0]["out_0_dram"]
```

```python
from contextlib import ExitStack

import concourse.bass as bass
from concourse import mybir

F32 = mybir.dt.float32
ALU = mybir.AluOpType
ACT = mybir.ActivationFunctionType
AX = mybir.AxisListType

B, N, C, R = 8, 2048, 64, 16
P = 128
SB = 512
KB = SB // P
NT = N // P
DEG_EPS = 1e-12
LN_EPS = 1e-5

UNITS = [(0, 1), (2, 3), (0, 2), (1, 3), (0, 3), (0, 0), (2, 2), (1, 1), (3, 3), (1, 2)]
DOUBLED = 2
SUPERUNITS = [[(0, 2)], [(1, 3)], [(0, 3)], [(0, 0), (2, 2)], [(1, 1), (3, 3)], [(1, 2)], [(0, 1), (2, 3)]]

W_SLOTS = 4
MIRROR_BANKS = 4
BACK_BANKS = 2
BACK_SLOTS = 4


def first_block(I, J, k):
    return k if I == J else 0


CHUNKS = [(u, I, J, k, P * first_block(I, J, k), SB - P * first_block(I, J, k))
          for u, (I, J) in enumerate(UNITS) for k in range(KB)]
NC = len(CHUNKS)


def places():
    a_at, s_at, at, end = {}, {}, 0, 0
    for u, I, J, k, _, width in CHUNKS:
        a_at[I, J, k] = at
        at += width
        for parity in range(2):
            if parity == 1 and u >= DOUBLED:
                s_at[1, I, J, k] = s_at[0, I, J, k]
            else:
                s_at[parity, I, J, k] = end
                end += width
    return a_at, s_at, at, end


A_AT, S_AT, A_COLS, S_COLS = places()


def loads():
    out = []
    for u, (I, J) in enumerate(UNITS):
        if I != J:
            out.append((J, I, u, True))
        out.append((I, J, u, False))
    return out


LOADS = loads()
NL = len(LOADS)
LOAD_OF = {(row, col): m for m, (row, col, _, _) in enumerate(LOADS)}
assert NL % W_SLOTS == 0

EARLY = 2
Y_BANK = [(EARLY + i) % MIRROR_BANKS for i in range(2)]
COL_BANK, DEG_BANK = ((NC + 2 + i) % MIRROR_BANKS for i in range(2))
assert (NC + 4) % MIRROR_BANKS == 0


def mirror_bank(c):
    return (c if c < EARLY else c + 2) % MIRROR_BANKS


FIRST_UNIT = {J: next((I, K) for I, K in UNITS if K == J) for J in range(N // SB)}
NCOL = sum(not (I == J and k == KB - 1) and not (k == 0 and FIRST_UNIT[J] == (I, J))
           for _, I, J, k, _, _ in CHUNKS) + sum(I == J for J, (I, _) in FIRST_UNIT.items())


def groups():
    out, n, ends, last = [], 0, {}, {}
    for superunit in SUPERUNITS:
        for k in range(KB):
            natural, back = [], []
            for I, J in superunit:
                natural.append((I, J, k))
                blocks = k if I == J else KB
                if blocks:
                    back.append((I, J, k, blocks, n))
                    n += 1
            if superunit[0][0] != superunit[0][1] and len(superunit) > 1:
                out += [(natural, []), ([], back)]
            else:
                out.append((natural, back))
        for unit in superunit:
            ends[unit], last[unit] = n, len(out) - 1
    return out, n, ends, last


GROUPS, NB, UNIT_DONE, UNIT_GROUP = groups()
assert NB % BACK_BANKS == 0 and NB % BACK_SLOTS == 0


def ends_of_sums():
    first, last = {}, {}
    for g, (natural, back_products) in enumerate(GROUPS):
        for kind, targets in (("natural", [J for _, J, _ in natural]), ("back", [b[0] for b in back_products])):
            for J in targets:
                first.setdefault(J, (g, kind))
                last[J] = (g, kind)
    return first, last


FIRST, LAST = ends_of_sums()

MEAN_AT, VARIANCE_AT = 7, 16
RESIDUAL_AT, CENTRE_AT, NORMALISE_AT = 2, 9, 18
SUM_AT, TURN_SUMS_AT = 28, 29
ROOT_AT, STORE_AT, COPY_SUMS_AT = 16, 32, 34
X_LOAD_AT = LOAD_OF[0, 0]

CHUNK_US, COLUMN_US = 0.14, 2.08e-3
TURN_US, PRODUCT_US = 0.109, 0.454
X_US, Y_US, TWO_CHUNKS_US = 1.3, 1.3, 2.2
AHEAD = 2


def tensor_order(mirrors, products):
    chunks = NC if mirrors else 0
    total = len(GROUPS) if products else 0
    order, c, g, now = [], 0, 0, 0.0
    done_at, starts = {}, []
    while c < chunks or g < total:
        while len(starts) < chunks:
            n = len(starts)
            start = starts[-1] + CHUNK_US + COLUMN_US * CHUNKS[n - 1][5] if n else X_US
            if n == EARLY:
                start += Y_US
            if total and CHUNKS[n][0] >= DOUBLED:
                gating = UNIT_GROUP[CHUNKS[n][1], CHUNKS[n][2]]
                if gating not in done_at:
                    break
                start = max(start, done_at[gating])
            starts.append(start)
        lag = TWO_CHUNKS_US if c < 2 * EARLY else 0.0
        ready = c < AHEAD or (c - AHEAD < len(starts) and starts[c - AHEAD] + lag <= now)
        if c < chunks and (g == total or ready):
            order.append(("mirror", c))
            now += TURN_US * CHUNKS[c][5] / P
            if c == EARLY - 1 and products:
                now += 1.3
            c += 1
        else:
            order.append(("group", g))
            natural, back_products = GROUPS[g]
            columns = sum(SB - P * first_block(*n) for n in natural) + sum(P * b[3] for b in back_products)
            now += PRODUCT_US * columns / SB + sum(TURN_US * b[3] for b in back_products)
            done_at[g] = now
            g += 1
    return order


def propagate(nc, x, adj, U, w_scale, out):
    with ExitStack() as ctx:
        def sbuf(name, shape):
            return ctx.enter_context(nc.sbuf_tensor(name, shape, F32))

        def psum(name, shape):
            return ctx.enter_context(nc.psum_tensor(name, shape, F32))

        def sem(name):
            return ctx.enter_context(nc.semaphore(name))

        a_store = sbuf("a_store", [P, A_COLS])
        s_store = sbuf("s_store", [P, S_COLS])
        w_ring = sbuf("w_ring", [P, W_SLOTS, KB, SB])
        back = sbuf("back", [P, BACK_SLOTS, SB])
        colacc = sbuf("colacc", [P, N])
        x_in = [sbuf(f"x_in{i}", [P, NT, C]) for i in range(2)]
        x_scaled = sbuf("x_scaled", [P, NT, C])
        y_t = sbuf("y_t", [P, 2, SB])
        res = sbuf("res", [P, NT, C])
        ident = sbuf("ident", [P, P])
        ones = sbuf("ones", [P, 32])
        row_sums = sbuf("row_sums", [P, NT, KB])
        row_sum = sbuf("row_sum", [P, NT])
        deg = sbuf("deg", [P, NT])
        deg_half = sbuf("deg_half", [P, NT])
        deg_inv = sbuf("deg_inv", [P, NT])
        d = sbuf("d", [P, NT])
        d_half = sbuf("d_half", [P, NT])
        d_scale = [sbuf(f"d_scale{i}", [P, NT]) for i in range(2)]
        w_col = sbuf("w_col", [P, 1])
        sums = sbuf("sums", [P, NT])
        neg_mean = sbuf("neg_mean", [P, NT])
        squares = sbuf("squares", [P, NT])
        var = sbuf("var", [P, NT])
        var_inv = sbuf("var_inv", [P, NT])
        rstd = sbuf("rstd", [P, NT])
        u_in = res[:, :, :].rearrange("p t c -> p (t c)")[:, 0:NT * R]
        u_t = back[0:R, :, :].rearrange("p s c -> p (s c)")
        col_sums = y_t[:, 0, :]
        square_of = y_t[:, :, :].rearrange("p s (t c) -> p (s t) c", c=C)

        y = psum("y", [P, 2, SB])
        mirror = psum("mirror", [P, MIRROR_BANKS, SB])
        turned = psum("turned", [P, BACK_BANKS, SB])

        w_landed = [sem(f"w_landed{i}") for i in range(W_SLOTS)]
        x_landed = [sem(f"x_landed{i}") for i in range(2)]
        u_landed = sem("u_landed")
        scale_landed = sem("scale_landed")
        out_stored = sem("out_stored")
        consts_ready = sem("consts_ready")
        ident_zero = sem("ident_zero")
        rows_clear = sem("rows_clear")
        u_turned = sem("u_turned")
        u_t_ready = sem("u_t_ready")
        a_logits = sem("a_logits")
        a_ready = sem("a_ready")
        mirrored = sem("mirrored")
        summed = sem("summed")
        s_ready = sem("s_ready")
        cols_added = sem("cols_added")
        col_summed = sem("col_summed")
        col_copied = sem("col_copied")
        deg_turned = sem("deg_turned")
        row_summed = sem("row_summed")
        deg_added = sem("deg_added")
        deg_bounded = sem("deg_bounded")
        d_halved = sem("d_halved")
        d_scaled = sem("d_scaled")
        inv_ready = sem("inv_ready")
        d_ready = sem("d_ready")
        x_ready = sem("x_ready")
        s_turned = sem("s_turned")
        back_ready = sem("back_ready")
        back_used = sem("back_used")
        y_copied = sem("y_copied")
        y_turned = sem("y_turned")
        y_scaled = sem("y_scaled")
        x_added = sem("x_added")
        row_added = sem("row_added")
        mean_ready = sem("mean_ready")
        centred = sem("centred")
        squared = sem("squared")
        squares_summed = sem("squares_summed")
        var_added = sem("var_added")
        var_ready = sem("var_ready")
        rstd_ready = sem("rstd_ready")
        normed = sem("normed")

        block = ctx.enter_context(nc.Block())

        def due(count):
            return not isinstance(count, int) or count > 0

        def col_part(parity, c):
            _, I, J, k, col0, width = CHUNKS[c]
            skip = P if I == J else 0
            if width == skip:
                return None
            at = S_AT[parity, I, J, k]
            return (col0 + skip, width - skip), s_store[:, at + skip:at + width]

        def x_count(p, parity):
            return (p - parity) * 8 + 16

        def lane(J):
            return slice(C * (J // 2), C * (J // 2) + C)

        def all_steps(eng, step):
            step(0, 0)
            step(1, 1)
            with eng.Fori(2, B - 1, 2) as b:
                step(b, 0)
                step(b + 1, 1)
            step(B, B % 2)
            step(B + 1, (B + 1) % 2)

        def has(b, lag):
            return not isinstance(b, int) or 0 <= b - lag < B

        @block.sync
        def _(sp):
            def step(b, parity):
                if not has(b, 0):
                    return
                for m, (row, col, u, _) in enumerate(LOADS):
                    before = (m - W_SLOTS) % NL
                    batch_before = b if m >= W_SLOTS else b - 1
                    if has(batch_before, 0):
                        last_chunk = KB * LOADS[before][2] + KB
                        if LOADS[before][3]:
                            sp.wait_ge(mirrored, batch_before * NC + last_chunk)
                        else:
                            sp.wait_ge(summed, batch_before * NC + last_chunk)
                    if m == X_LOAD_AT:
                        sp.dma_start(x_in[parity][:, :, :],
                                     x[bass.ds(b, 1), :, :].rearrange("o (t p) c -> p (o t) c", p=P))\
                            .then_inc(x_landed[parity], 16)
                    sp.dma_start(w_ring[:, m % W_SLOTS, :, :],
                                 adj[bass.ds(b, 1), row * SB:(row + 1) * SB, col * SB:(col + 1) * SB]
                                 .rearrange("o (k p) c -> p (o k) c", p=P)).then_inc(w_landed[m % W_SLOTS], 16)

            all_steps(sp, step)
            sp.wait_ge(out_stored, 16 * B)

        @block.gpsimd
        def _(pool):
            pool.memset(ident[:, :], 0.0).then_inc(ident_zero, 1)
            pool.memset(ones[:, :], 1.0).then_inc(consts_ready, 1)
            pool.wait_ge(ident_zero, 1)
            pool.affine_select(out=ident[:, :], in_=ident[:, :], compare_op=ALU.not_equal, fill=1.0, base=0,
                               pattern=[[-1, P]], channel_multiplier=1).then_inc(consts_ready, 1)

            pool.memset(colacc[:, 0:P], 0.0).then_inc(consts_ready, 1)

            def residual(q, parity):
                pool.wait_ge(y_scaled, 2 * q + 2)
                pool.tensor_tensor(res[:, :, :], res[:, :, :], x_in[parity][:, :, :], ALU.add).then_inc(x_added, 1)

            def by_row(values):
                return values[:, :].rearrange("p (t o) -> p t o", o=1).broadcast_to([P, NT, C])

            def centre(q):
                pool.wait_ge(mean_ready, q + 1)
                pool.tensor_tensor(res[:, :, :], res[:, :, :], by_row(neg_mean), ALU.add).then_inc(centred, 1)
                pool.wait_ge(centred, q + 1)
                pool.wait_ge(y_turned, 2 * q + 2)
                pool.tensor_tensor(square_of, res[:, :, :], res[:, :, :], ALU.mult).then_inc(squared, 1)

            def normalise(q):
                pool.wait_ge(rstd_ready, q + 1)
                pool.tensor_tensor(res[:, :, :], res[:, :, :], by_row(rstd), ALU.mult).then_inc(normed, 1)

            def step(b, parity):
                q = b - 2
                if not has(b, 0):
                    if has(b, 2):
                        residual(q, parity)
                        centre(q)
                        normalise(q)
                    return
                if due(count := b):
                    pool.wait_ge(col_summed, count)
                done = 0
                for c, (_, I, J, k, _, _) in enumerate(CHUNKS):
                    if has(b, 2):
                        if c == RESIDUAL_AT + 1:
                            residual(q, parity)
                        if c == CENTRE_AT + 1:
                            centre(q)
                        if c == NORMALISE_AT + 1:
                            normalise(q)
                    part = col_part(parity, c)
                    if part is None or (k == 0 and FIRST_UNIT[J] == (I, J)):
                        continue
                    (first, width), chunk = part
                    acc = colacc[:, J * SB + first:J * SB + SB]
                    pool.wait_ge(s_ready, b * NC + c + 1)
                    if k == 1 and FIRST_UNIT[J] == (I, J):
                        (first0, width0), chunk0 = col_part(parity, c - 1)
                        pool.tensor_tensor(acc, chunk0[:, width0 - width:width0], chunk, ALU.add)\
                            .then_inc(cols_added, 1)
                        if first0 < first:
                            pool.tensor_copy(colacc[:, J * SB + first0:J * SB + first], chunk0[:, 0:width0 - width])\
                                .then_inc(cols_added, 1)
                            done += 1
                    else:
                        if due(count := b * NCOL + done):
                            pool.wait_ge(cols_added, count)
                        pool.tensor_tensor(acc, acc, chunk, ALU.add).then_inc(cols_added, 1)
                    done += 1
                assert done == NCOL

            all_steps(pool, step)

        @block.vector
        def _(dve):
            dve.memset(row_sums[:, :, :], 0.0).then_inc(rows_clear, 1)
            dve.wait_ge(rows_clear, 1)
            dve.wait_ge(scale_landed, 16)

            def add_mirror(b, c):
                _, I, J, k, col0, width = CHUNKS[c]
                m = LOAD_OF[I, J]
                dve.wait_ge(mirrored, b * NC + c + 1)
                if k == 0:
                    dve.wait_ge(w_landed[m % W_SLOTS], 16 * (b * (NL // W_SLOTS) + m // W_SLOTS + 1))
                bank = mirror[:, mirror_bank(c), 0:width]
                dve.tensor_tensor(bank, bank, w_ring[:, m % W_SLOTS, k, col0:SB], ALU.add).then_inc(summed, 1)

            def times_a(b, parity, c):
                u, I, J, k, col0, width = CHUNKS[c]
                dve.wait_ge(summed, b * NC + c + 1)
                if isinstance(b, int) and b == 0:
                    dve.wait_ge(a_ready, c + 1)
                if k == 0:
                    if u >= DOUBLED:
                        if due(count := (b - 1) * NB + UNIT_DONE[I, J]):
                            dve.wait_ge(back_used, count)
                    elif u == 0:
                        if due(count := (b - 1) * NB):
                            dve.wait_ge(back_used, count)
                at, a0 = S_AT[parity, I, J, k], A_AT[I, J, k]
                dve.scalar_tensor_tensor(out=s_store[:, at:at + width], in0=mirror[:, mirror_bank(c), 0:width],
                                         scalar=1.0, in1=a_store[:, a0:a0 + width], op0=ALU.mult, op1=ALU.mult,
                                         accum_out=row_sums[:, KB * I + k, J:J + 1]).then_inc(s_ready, 1)

            def degrees(p):
                dve.wait_ge(s_ready, (p + 1) * NC)
                dve.tensor_reduce(out=row_sum[:, :], in_=row_sums[:, :, :], axis=AX.X, op=ALU.add)\
                    .then_inc(row_summed, 1)
                dve.wait_ge(row_summed, p + 1)
                dve.wait_ge(deg_turned, p + 1)
                by_node = mirror[:, DEG_BANK, :].rearrange("p (k j q) -> p j k q", k=KB, j=KB)[:, :, :, 0]
                dve.tensor_tensor(deg[:, :].rearrange("p (j k) -> p j k", j=KB), by_node,
                                  row_sum[:, :].rearrange("p (j k) -> p j k", j=KB), ALU.add).then_inc(deg_added, 1)
                dve.wait_ge(deg_added, p + 1)
                dve.tensor_scalar(deg_half[:, :], deg[:, :], 0.5, DEG_EPS, ALU.mult, ALU.max).then_inc(deg_bounded, 1)
                dve.wait_ge(deg_bounded, p + 1)
                dve.reciprocal(deg_inv[:, :], deg_half[:, :]).then_inc(inv_ready, 1)

            def scale_x(p, parity):
                dve.wait_ge(d_ready, p + 1)
                dve.tensor_scalar(d_half[:, :], d[:, :], 0.5, None, ALU.mult).then_inc(d_halved, 1)
                dve.tensor_scalar(d_scale[parity][:, :], d[:, :], w_col[:, 0:1], None, ALU.mult).then_inc(d_scaled, 1)
                dve.wait_ge(d_halved, p + 1)
                dve.wait_ge(x_landed[parity], x_count(p, parity))
                if due(count := p * NB):
                    dve.wait_ge(back_used, count)
                dve.tensor_tensor(x_scaled[:, :, :], x_in[parity][:, :, :],
                                  d_half[:, :].rearrange("p (t o) -> p t o", o=1).broadcast_to([P, NT, C]), ALU.mult)\
                    .then_inc(x_ready, 1)

            def scale_y(q, parity, bank):
                dve.wait_ge(y_turned, 2 * q + bank + 1)
                if bank == 0:
                    if due(count := 16 * q):
                        dve.wait_ge(out_stored, count)
                    dve.wait_ge(d_scaled, q + 1)
                scale = d_scale[parity][:, :].rearrange("p (l s k o) -> p l s k o", l=2, s=2, o=1)[:, :, bank]
                dve.tensor_tensor(
                    res[:, :, :].rearrange("p (l s k) c -> p l s k c", l=2, s=2)[:, :, bank],
                    mirror[:, Y_BANK[bank], :].rearrange("p (k l c) -> p l k c", k=KB, l=2),
                    scale.broadcast_to([P, 2, KB, C]), ALU.mult).then_inc(y_scaled, 1)

            def mean(q):
                dve.wait_ge(x_added, q + 1)
                dve.tensor_reduce(out=sums[:, :], in_=res[:, :, :], axis=AX.X, op=ALU.add).then_inc(row_added, 1)
                dve.wait_ge(row_added, q + 1)
                dve.tensor_scalar(neg_mean[:, :], sums[:, :], -1.0 / C, None, ALU.mult).then_inc(mean_ready, 1)

            def variance(q):
                dve.wait_ge(squared, q + 1)
                dve.tensor_reduce(out=squares[:, :], in_=square_of, axis=AX.X, op=ALU.add).then_inc(squares_summed, 1)
                dve.wait_ge(squares_summed, q + 1)
                dve.tensor_scalar(var[:, :], squares[:, :], 1.0 / C, LN_EPS, ALU.mult, ALU.add).then_inc(var_added, 1)
                dve.wait_ge(var_added, q + 1)
                dve.reciprocal(var_inv[:, :], var[:, :]).then_inc(var_ready, 1)

            def step(b, parity):
                p, q = b - 1, b - 2
                if has(b, 1):
                    scale_x(p, 1 - parity)
                if has(b, 0):
                    add_mirror(b, 0)
                for c in range(NC):
                    if has(b, 0):
                        if c + 1 < NC:
                            add_mirror(b, c + 1)
                        times_a(b, parity, c)
                    if c == EARLY - 1 and has(b, 2):
                        scale_y(q, parity, 0)
                        scale_y(q, parity, 1)
                    if c == MEAN_AT and has(b, 2):
                        mean(q)
                    if c == VARIANCE_AT and has(b, 2):
                        variance(q)
                if has(b, 0):
                    degrees(b)

            all_steps(dve, step)

        @block.scalar
        def _(act):
            act.dma_start(u_in, U.rearrange("(p t) r -> p (t r)", p=P)).then_inc(u_landed, 16)
            act.dma_start(w_col[:, :], w_scale.partition_broadcast(P)).then_inc(scale_landed, 16)
            by_tile = u_t.rearrange("r (p t) -> r t p", t=NT)
            act.wait_ge(u_turned, 1)
            act.activation(by_tile[:, 0:NT // 2, :], y[0:R, :, :].rearrange("r s (t p) -> r (s t) p", p=P), ACT.Copy)\
                .then_inc(u_t_ready, 1)
            act.activation(by_tile[:, NT // 2:NT, :], turned[0:R, :, :].rearrange("r s (t p) -> r (s t) p", p=P),
                           ACT.Copy).then_inc(u_t_ready, 1)
            for c, (_, I, J, k, _, width) in enumerate(CHUNKS):
                act.wait_ge(a_logits, c + 1)
                a0 = A_AT[I, J, k]
                act.activation(a_store[:, a0:a0 + width], turned[:, c % BACK_BANKS, 0:width], ACT.Sigmoid)\
                    .then_inc(a_ready, 1)

            def copy_y(q):
                if due(count := 2 * q):
                    act.wait_ge(y_turned, count)
                if due(count := q):
                    act.wait_ge(squares_summed, count)
                if has(q, -1):
                    act.wait_ge(deg_turned, q + 2)
                act.wait_ge(back_used, (q + 1) * NB)
                for bank in range(2):
                    act.activation(y_t[:, bank, :], y[:, bank, :], ACT.Copy).then_inc(y_copied, 1)

            def copy_column_sums(p):
                if due(count := p - 1):
                    act.wait_ge(squares_summed, count)
                act.wait_ge(col_summed, p + 1)
                act.activation(col_sums, mirror[:, COL_BANK, :], ACT.Copy).then_inc(col_copied, 1)

            def root_degrees(p):
                act.wait_ge(inv_ready, p + 1)
                act.activation(d[:, :], deg_inv[:, :], ACT.Sqrt).then_inc(d_ready, 1)

            def copy_back(p, n, blocks):
                act.wait_ge(s_turned, p * NB + n + 1)
                if due(count := p * NB + n + 1 - BACK_SLOTS):
                    act.wait_ge(back_used, count)
                act.activation(back[:, n % BACK_SLOTS, 0:P * blocks], turned[:, n % BACK_BANKS, 0:P * blocks],
                               ACT.Copy).then_inc(back_ready, 1)

            def root_variance(q):
                act.wait_ge(var_ready, q + 1)
                act.activation(rstd[:, :], var_inv[:, :], ACT.Sqrt).then_inc(rstd_ready, 1)

            def store(q):
                act.wait_ge(normed, q + 1)
                act.dma_start(out[bass.ds(q, 1), :, :].rearrange("o (t p) c -> p (o t) c", p=P), res[:, :, :])\
                    .then_inc(out_stored, 16)

            def step(b, parity):
                p, q = b - 1, b - 2
                if has(b, 2):
                    copy_y(q)
                for _, back_products in GROUPS:
                    for _, _, _, blocks, n in back_products:
                        if n == COPY_SUMS_AT and has(b, 0):
                            copy_column_sums(b)
                        if has(b, 1):
                            copy_back(p, n, blocks)
                        if n == ROOT_AT and has(b, 2):
                            root_variance(q)
                        if n == STORE_AT and has(b, 2):
                            store(q)
                if has(b, 0):
                    root_degrees(b)

            all_steps(act, step)

        @block.tensor
        def _(pe):
            pe.wait_ge(consts_ready, 3)
            pe.wait_ge(u_landed, 16)
            for t in range(NT):
                bank = y if t < NT // 2 else turned
                last = pe.transpose(bank[0:R, t // KB % 2, P * (t % KB):P * (t % KB) + P], u_in[:, R * t:R * t + R],
                                    ident[:, :])
            last.then_inc(u_turned, 1)
            pe.wait_ge(u_t_ready, 2)

            def logits(c):
                _, I, J, k, col0, width = CHUNKS[c]
                if c >= BACK_BANKS:
                    pe.wait_ge(a_ready, c + 1 - BACK_BANKS)
                row = I * SB + k * P
                pe.matmul(turned[:, c % BACK_BANKS, 0:width], u_t[:, row:row + P],
                          u_t[:, J * SB + col0:J * SB + SB], start=True, stop=True).then_inc(a_logits, 1)

            def turn_mirror(b, c):
                _, I, J, k, col0, _ = CHUNKS[c]
                m = LOAD_OF[J, I]
                if k == 0:
                    pe.wait_ge(w_landed[m % W_SLOTS], 16 * (b * (NL // W_SLOTS) + m // W_SLOTS + 1))
                if EARLY + 2 <= c < EARLY + 4:
                    if has(b, 2):
                        pe.wait_ge(y_scaled, 2 * (b - 2) + c - EARLY - 1)
                else:
                    chunk_before = c - (2 if c < EARLY + 2 else MIRROR_BANKS)
                    if due(count := b * NC + chunk_before + 1):
                        pe.wait_ge(s_ready, count)
                for j in range(col0 // P, KB):
                    last = pe.transpose(mirror[:, mirror_bank(c), P * j - col0:P * j - col0 + P],
                                        w_ring[:, m % W_SLOTS, j, P * k:P * k + P], ident[:, :])
                last.then_inc(mirrored, 1)

            def sum_columns(p):
                pe.wait_ge(cols_added, (p + 1) * NCOL)
                pe.wait_ge(s_ready, (p + 1) * NC)
                for J in range(KB):
                    last = pe.matmul(mirror[32 * J:32 * J + 32, COL_BANK, :], ones[:, :], colacc[:, J * SB:J * SB + SB],
                                     start=True, stop=True)
                last.then_inc(col_summed, 1)

            def turn_column_sums(p):
                pe.wait_ge(col_copied, p + 1)
                for k in range(KB):
                    last = pe.transpose(mirror[:, DEG_BANK, P * k:P * k + P], col_sums[:, P * k:P * k + P], ident[:, :])
                last.then_inc(deg_turned, 1)

            def turn_y(q, bank):
                pe.wait_ge(y_copied, 2 * q + bank + 1)
                if bank == 1 and has(q, -1):
                    pe.wait_ge(deg_added, q + 2)
                for k in range(KB):
                    last = pe.transpose(mirror[:, Y_BANK[bank], P * k:P * k + P], y_t[:, bank, P * k:P * k + P], ident[:, :])
                last.then_inc(y_turned, 1)

            def turn_back(p, parity, I, J, k, blocks, n):
                if due(count := p * NB + n + 1 - BACK_BANKS):
                    pe.wait_ge(back_ready, count)
                for i in range(blocks):
                    at = S_AT[parity, I, J, i] + P * (k - first_block(I, J, i))
                    last = pe.transpose(turned[:, n % BACK_BANKS, P * i:P * i + P], s_store[:, at:at + P], ident[:, :])
                last.then_inc(s_turned, 1)

            def group_turns(p, parity, g):
                for I, J, k, blocks, n in GROUPS[g][1]:
                    turn_back(p, parity, I, J, k, blocks, n)

            def group_products(p, parity, g):
                natural, back_products = GROUPS[g]
                for I, J, k in natural:
                    at, block0 = S_AT[parity, I, J, k], first_block(I, J, k)
                    pe.matmul(y[lane(J), J % 2, P * block0:SB], x_scaled[:, KB * I + k, :],
                              s_store[:, at:at + SB - P * block0], start=FIRST[J] == (g, "natural"),
                              stop=LAST[J] == (g, "natural"))
                for I, J, k, blocks, n in back_products:
                    pe.wait_ge(back_ready, p * NB + n + 1)
                    pe.matmul(y[lane(I), I % 2, 0:P * blocks], x_scaled[:, KB * J + k, :],
                              back[:, n % BACK_SLOTS, 0:P * blocks], start=FIRST[I] == (g, "back"),
                              stop=LAST[I] == (g, "back")).then_inc(back_used, 1)

            def step(b, parity):
                p, q = b - 1, b - 2
                if has(b, 0) and not has(b, 1):
                    logits(0)
                    logits(1)
                order = tensor_order(has(b, 0), has(b, 1))
                if not has(b, 0) and has(b, 2):
                    turn_y(q, 0)
                    turn_y(q, 1)
                for kind, n in order:
                    if kind == "mirror":
                        if not has(b, 1) and n + 2 < NC:
                            logits(n + 2)
                        turn_mirror(b, n)
                        if n == EARLY - 1:
                            if has(b, 1):
                                group_turns(p, 1 - parity, 0)
                            if has(b, 2):
                                turn_y(q, 0)
                                turn_y(q, 1)
                    if kind == "group":
                        if n == 0:
                            if not has(b, 0):
                                group_turns(p, 1 - parity, 0)
                            pe.wait_ge(x_ready, p + 1)
                            if due(count := 2 * p):
                                pe.wait_ge(y_copied, count)
                        if n + 1 < len(GROUPS):
                            group_turns(p, 1 - parity, n + 1)
                        group_products(p, 1 - parity, n)
                    if has(b, 0):
                        if (kind, n) == (("group", SUM_AT) if has(b, 1) else order[-1]):
                            assert ("mirror", NC - 1) in order[:order.index((kind, n)) + 1]
                            sum_columns(b)
                        if (kind, n) == (("group", TURN_SUMS_AT) if has(b, 1) else order[-1]):
                            turn_column_sums(b)

            all_steps(pe, step)


_INS = ["x", "adj", "L0_gnn_U", "L0_gnn_w_scale"]


def kernel(**inputs):
    import numpy as _np
    import concourse.bacc as _bacc
    from concourse import mybir as _mybir
    from concourse.bass_utils import run_bass_kernel_spmd as _run

    nc = _bacc.Bacc("TRN2", target_bir_lowering=False, num_devices=1, dynamic_dma_scratch_size=1024)
    arrays, args = {}, []
    for name in _INS:
        a = _np.ascontiguousarray(inputs[name])
        if a.ndim == 0:
            a = a.reshape(1)
        arrays[f"in_{name}_dram"] = a
        args.append(nc.dram_tensor(f"in_{name}_dram", a.shape, _mybir.dt.from_np(a.dtype), kind="ExternalInput").ap())
    out = nc.dram_tensor("out_0_dram", (B, N, C), _mybir.dt.float32, kind="ExternalOutput").ap()
    propagate(nc, *args, out)
    r = _run(nc, [arrays], core_ids=[0])
    return r.results[0]["out_0_dram"]
```

```python
from contextlib import ExitStack

import concourse.bass as bass
from concourse import mybir

F32 = mybir.dt.float32
BF16 = mybir.dt.bfloat16
ALU = mybir.AluOpType
ACT = mybir.ActivationFunctionType
AX = mybir.AxisListType

B, N, C, R = 8, 2048, 64, 16
P = 128
SB = 512
KB = SB // P
NT = N // P
PARTS = 3
DEG_EPS = 1e-12
LN_EPS = 1e-5

UNITS = [(0, 1), (2, 3), (0, 2), (1, 3), (0, 3), (0, 0), (2, 2), (1, 1), (3, 3), (1, 2)]
DOUBLED = 2
def both(*units):
    return [(list(units), list(units))]


STAGES = [both((0, 2)), both((1, 3)), both((0, 3)), both((0, 0), (2, 2)), both((1, 1), (3, 3)), both((1, 2)),
          [([(0, 1), (2, 3)], []), ([], [(0, 1), (2, 3)])]]
END_STAGES = [both((0, 2)), both((0, 0), (2, 2)), [([], [(0, 1), (2, 3)])], [([(1, 2)], [(0, 3)])],
              both((1, 3)), both((1, 1), (3, 3)), [([(0, 1), (2, 3)], [])], [([(0, 3)], [(1, 2)])]]
END_FIRST_HALF = 4

W_SLOTS = 4
MIRROR_BANKS = 4
BACK_BANKS = 2
BACK_SLOTS = 4


def first_block(I, J, k):
    return k if I == J else 0


CHUNKS = [(u, I, J, k, P * first_block(I, J, k), SB - P * first_block(I, J, k))
          for u, (I, J) in enumerate(UNITS) for k in range(KB)]
NC = len(CHUNKS)


def places():
    a_at, s_at, at, end = {}, {}, 0, 0
    for u, I, J, k, _, width in CHUNKS:
        a_at[I, J, k] = at
        at += width
        for parity in range(2):
            if parity == 1 and u >= DOUBLED:
                s_at[1, I, J, k] = s_at[0, I, J, k]
            else:
                s_at[parity, I, J, k] = end
                end += width
    return a_at, s_at, at, end


A_AT, S_AT, A_COLS, S_COLS = places()


def loads():
    out = []
    for u, (I, J) in enumerate(UNITS):
        if I != J:
            out.append((J, I, u, True))
        out.append((I, J, u, False))
    return out


LOADS = loads()
NL = len(LOADS)
LOAD_OF = {(row, col): m for m, (row, col, _, _) in enumerate(LOADS)}
assert NL % W_SLOTS == 0

EARLY = 4
RING = [("chunk", c) for c in range(EARLY)] + [("y", 0), ("y", 1)] + [("chunk", c) for c in range(EARLY, NC)]\
    + [("column sums", 0), ("degrees", 0)]
assert len(RING) % MIRROR_BANKS == 0


def ring_bank(what, n=0):
    return RING.index((what, n)) % MIRROR_BANKS


def ring_before(what, n=0):
    at = RING.index((what, n)) - MIRROR_BANKS
    return (*RING[at], at < 0)


Y_BANK = [ring_bank("y", i) for i in range(2)]
COL_BANK, DEG_BANK = ring_bank("column sums"), ring_bank("degrees")


def mirror_bank(c):
    return ring_bank("chunk", c)


FIRST_UNIT = {J: next((I, K) for I, K in UNITS if K == J) for J in range(N // SB)}
NCOL = sum(not (I == J and k == KB - 1) and not (k == 0 and FIRST_UNIT[J] == (I, J))
           for _, I, J, k, _, _ in CHUNKS) + sum(I == J for J, (I, _) in FIRST_UNIT.items())


PE_SUMS = [NC - 3, NC - 2, NC - 1]
assert all(CHUNKS[c][1] != CHUNKS[c][2] for c in PE_SUMS)


def groups(stages):
    out, n, ends, last = [], 0, {}, {}
    for stage in stages:
        for k in range(KB):
            for natural_units, back_units in stage:
                back = []
                for I, J in back_units:
                    blocks = k if I == J else KB
                    if blocks:
                        back.append((I, J, k, blocks, n))
                        n += 1
                out.append(([(I, J, k) for I, J in natural_units], back))
        for natural_units, back_units in stage:
            for unit in natural_units + back_units:
                ends[unit], last[unit] = n, len(out) - 1
    return out, n, ends, last


GROUPS, NB, UNIT_DONE, UNIT_GROUP = groups(STAGES)
END_GROUPS, end_count, _, _ = groups(END_STAGES)
END_HALF_GROUP = KB * END_FIRST_HALF - 1
END_HALF_DONE = groups(END_STAGES[:END_FIRST_HALF])[1]
assert end_count == NB
assert NB % BACK_BANKS == 0 and NB % BACK_SLOTS == 0


def ends_of_sums(groups):
    first, last = {}, {}
    for g, (natural, back_products) in enumerate(groups):
        for kind, targets in (("natural", [J for _, J, _ in natural]), ("back", [b[0] for b in back_products])):
            for J in targets:
                first.setdefault(J, (g, kind))
                last[J] = (g, kind)
    return first, last


def first_odd(groups):
    with_x = [g for g, (natural, back) in enumerate(groups)
              if any(I % 2 for I, _, _ in natural) or any(product[1] % 2 for product in back)]
    into_y = [g for g, (natural, back) in enumerate(groups)
              if any(J % 2 for _, J, _ in natural) or any(product[0] % 2 for product in back)]
    return with_x[0], into_y[0]


SCALE_Y_AT, MEAN_AT, VARIANCE_AT = 3, 7, 16
RESIDUAL_AT, CENTRE_AT, NORMALISE_AT = 2, 9, 18
Y_TURN_AT, SUM_AT, TURN_SUMS_AT = (0, 1), 28, 29
END_TURN_LAG = 2
FIRST_TURNS_AT = 0
COPY_Y_AT, ROOT_AT, STORE_AT, COPY_SUMS_AT = 0, 16, 32, 34
END_STORE_AT = 18
END_COPY_AT, END_SQUARE_AT, END_ROOT_AT, END_HALF_STORE_AT = (END_HALF_DONE + i for i in (1, 5, 7, 9))
X_LOAD_AT = LOAD_OF[0, 0]

CHUNK_US, COLUMN_US = 0.14, 2.08e-3
TURN_US, PRODUCT_US = 0.109, 0.454
X_US, Y_US, TWO_CHUNKS_US = 0.6, 1.3, 2.0
LAG_US = 1.1
AHEAD = 2


def tensor_order(mirrors, products):
    chunks = NC if mirrors else 0
    groups = GROUPS if mirrors else END_GROUPS
    total = len(groups) if products else 0
    order, c, g, now = [], 0, 0, 0.0
    done_at, starts = {}, []
    while c < chunks or g < total:
        while len(starts) < chunks:
            n = len(starts)
            start = starts[-1] + CHUNK_US + COLUMN_US * CHUNKS[n - 1][5] if n else X_US
            if n == SCALE_Y_AT + 1:
                start += Y_US
            if total and CHUNKS[n][0] >= DOUBLED:
                gating = UNIT_GROUP[CHUNKS[n][1], CHUNKS[n][2]]
                if gating not in done_at:
                    break
                start = max(start, done_at[gating])
            starts.append(start)
        lag = TWO_CHUNKS_US if c < EARLY + 2 else LAG_US
        ready = c < EARLY or (c - AHEAD < len(starts) and starts[c - AHEAD] + lag <= now)
        if c < chunks and (g == total or ready):
            order.append(("mirror", c))
            now += TURN_US * CHUNKS[c][5] / P
            c += 1
        else:
            order.append(("group", g))
            natural, back_products = groups[g]
            columns = sum(SB - P * first_block(*n) for n in natural) + sum(P * b[3] for b in back_products)
            now += PRODUCT_US * columns / SB + sum(TURN_US * b[3] for b in back_products)
            if g in Y_TURN_AT:
                now += KB * TURN_US
            done_at[g] = now
            g += 1
    return order


def propagate(nc, x, adj, U, w_scale, out):
    with ExitStack() as ctx:
        def sbuf(name, shape):
            return ctx.enter_context(nc.sbuf_tensor(name, shape, F32))

        def psum(name, shape):
            return ctx.enter_context(nc.psum_tensor(name, shape, F32))

        def sem(name):
            return ctx.enter_context(nc.semaphore(name))

        a_store = sbuf("a_store", [P, A_COLS])
        s_store = sbuf("s_store", [P, S_COLS])
        w_ring = sbuf("w_ring", [P, W_SLOTS, KB, SB])
        back = sbuf("back", [P, BACK_SLOTS, SB])
        colacc = sbuf("colacc", [P, N])
        x_in = [sbuf(f"x_in{i}", [P, NT, C]) for i in range(2)]
        x_scaled = sbuf("x_scaled", [P, NT, C])
        y_t = sbuf("y_t", [P, 2, SB])
        res = sbuf("res", [P, NT, C])
        ident = sbuf("ident", [P, P])
        ones = sbuf("ones", [P, 32])
        row_sums = sbuf("row_sums", [P, NT, KB])
        row_sum = sbuf("row_sum", [P, NT])
        deg = sbuf("deg", [P, NT])
        deg_half = sbuf("deg_half", [P, NT])
        deg_inv = sbuf("deg_inv", [P, NT])
        d = sbuf("d", [P, NT])
        d_half = sbuf("d_half", [P, NT])
        d_scale = [sbuf(f"d_scale{i}", [P, NT]) for i in range(2)]
        w_col = sbuf("w_col", [P, 1])
        sums = sbuf("sums", [P, NT])
        neg_mean = sbuf("neg_mean", [P, NT])
        squares = sbuf("squares", [P, NT])
        var = sbuf("var", [P, NT])
        var_inv = sbuf("var_inv", [P, NT])
        rstd = sbuf("rstd", [P, NT])
        u_left = [res[:, :, :].rearrange("p t c -> p (t c)")[:, NT * R * i:NT * R * i + NT * R]
                  .rearrange("p (t r) -> p t r", t=NT) for i in range(3)]
        u_in = u_left[0]
        u_left_side, u_right_side, u_right_low = (
            s_store[:, PARTS * NT * R * i:PARTS * NT * R * i + groups * NT * R // 2].bitcast(BF16)
            .rearrange("p (t g r) -> p t g r", t=NT, r=R) for i, groups in enumerate((2 * PARTS, 2 * PARTS, PARTS)))
        u_t_left, u_t_right, u_t_low = (place.rearrange("p s c -> p (s c)").bitcast(BF16)
                                        for place in (back[:, 0:2, :], back[:, 2:4, :], y_t[:, :, :]))
        ident_bf16 = colacc[:, N - P // 2:N].bitcast(BF16)
        col_sums = y_t[:, 0, :]
        square_of = y_t[:, :, :].rearrange("p s (t c) -> p (s t) c", c=C)

        end_res, end_square = (w_ring[:, i, 0:2, :].rearrange("p k (t c) -> p (k t) c", c=C) for i in range(2))

        y = psum("y", [P, 2, SB])
        mirror = psum("mirror", [P, MIRROR_BANKS, SB])
        turned = psum("turned", [P, BACK_BANKS, SB])

        w_landed = [[sem(f"w_landed{i}_{h}") for h in range(2)] for i in range(W_SLOTS)]
        x_landed = [sem(f"x_landed{i}") for i in range(2)]
        u_landed = sem("u_landed")
        left_ready = sem("left_ready")
        right_ready = sem("right_ready")
        rest_ready = sem("rest_ready")
        scale_landed = sem("scale_landed")
        out_stored = sem("out_stored")
        end_stored = sem("end_stored")
        consts_ready = sem("consts_ready")
        ident_zero = sem("ident_zero")
        table_loaded = sem("table_loaded")
        ident_ready = sem("ident_ready")
        u_turned = sem("u_turned")
        u_t_ready = sem("u_t_ready")
        a_logits = sem("a_logits")
        a_ready = sem("a_ready")
        mirrored = sem("mirrored")
        summed = sem("summed")
        s_ready = sem("s_ready")
        cols_added = sem("cols_added")
        col_summed = sem("col_summed")
        col_copied = sem("col_copied")
        deg_turned = sem("deg_turned")
        row_summed = sem("row_summed")
        deg_added = sem("deg_added")
        deg_bounded = sem("deg_bounded")
        d_halved = sem("d_halved")
        d_scaled = sem("d_scaled")
        inv_ready = sem("inv_ready")
        d_ready = sem("d_ready")
        x_ready = sem("x_ready")
        s_turned = sem("s_turned")
        back_ready = sem("back_ready")
        back_used = sem("back_used")
        y_copied = sem("y_copied")
        y_turned = sem("y_turned")
        y_scaled = sem("y_scaled")
        x_added = sem("x_added")
        row_added = sem("row_added")
        mean_ready = sem("mean_ready")
        centred = sem("centred")
        squared = sem("squared")
        squares_summed = sem("squares_summed")
        var_added = sem("var_added")
        var_ready = sem("var_ready")
        rstd_ready = sem("rstd_ready")
        normed = sem("normed")
        (end_scaled, end_added, end_summed, end_mean, end_centred, end_squared, end_squares, end_var, end_inv, end_root,
         end_normed) = (sem(f"end_{what}") for what in ("scaled", "added", "summed", "mean", "centred", "squared", "squares",
                                                        "var", "inv", "root", "normed"))

        block = ctx.enter_context(nc.Block())

        def due(count):
            return not isinstance(count, int) or count > 0

        def half(values, bank):
            return values[:, :].rearrange("p (l s k) -> p l s k", l=2, s=2)[:, :, bank]

        def half_rows(values, bank):
            return values.rearrange("p (l s k) c -> p l s k c", l=2, s=2)[:, :, bank]

        def logit_bank(c):
            return (y if c % 4 < 2 else turned)[:, c % 2, :]

        def node_pairs(rows):
            return rows.rearrange("o (h p two) c -> p (o h) two c", p=P, two=2)

        def in_pairs(blocks):
            return blocks.rearrange("p (h two) c -> p h two c", two=2)

        def w_pairs(m, row_block, first, end):
            if first % 2 == 1:
                assert end == first + 1
                first_pair = first - 1
            else:
                first_pair = first
            pairs = w_ring[:, m % W_SLOTS, row_block, P * first_pair:P * (end + end % 2)]\
                .rearrange("p (h q two) -> p h two q", two=2, q=P)
            return pairs if (end - first) % 2 == 0 else pairs[:, 0, first % 2, :]

        def times(values, copies):
            return values.rearrange("p t (o r) -> p t o r", o=1).broadcast_to([P, NT, copies, R])

        def half_of_u(u_t, i, parts):
            return u_t[0:parts * R, N // 2 * i:N // 2 * (i + 1)]

        def turned_u(banks, bank, parts):
            return banks[0:parts * R, bank, :].bitcast(BF16)

        def col_part(parity, c):
            _, I, J, k, col0, width = CHUNKS[c]
            skip = P if I == J else 0
            if width == skip:
                return None
            at = S_AT[parity, I, J, k]
            return (col0 + skip, width - skip), s_store[:, at + skip:at + width]

        def x_count(p, parity):
            return (p - parity) * 8 + 16

        def cols_count(b, done):
            return b * NCOL + done - (len(PE_SUMS) if has(b, 1) else 0)

        def lane(J):
            return slice(C * (J // 2), C * (J // 2) + C)

        def all_steps(eng, step):
            step(0, 0)
            step(1, 1)
            with eng.Fori(2, B - 1, 2) as b:
                step(b, 0)
                step(b + 1, 1)
            step(B, B % 2)
            step(B + 1, (B + 1) % 2)

        def has(b, lag):
            return not isinstance(b, int) or 0 <= b - lag < B

        @block.sync
        def _(sp):
            sp.dma_start(in_pairs(u_in), U.rearrange("(h p two) r -> p h two r", p=P, two=2)).then_inc(u_landed, 16)

            def load_x(b, parity):
                sp.dma_start(in_pairs(x_in[parity][:, :, :]), node_pairs(x[bass.ds(b, 1), :, :]))\
                    .then_inc(x_landed[parity], 16)

            def step(b, parity):
                if not has(b, 0):
                    return
                for m, (row, col, u, _) in enumerate(LOADS):
                    before = (m - W_SLOTS) % NL
                    batch_before = b if m >= W_SLOTS else b - 1
                    _, _, unit_before, mirror_before = LOADS[before]
                    for h in range(2):
                        if has(batch_before, 0):
                            if mirror_before:
                                sp.wait_ge(mirrored, batch_before * NC + KB * unit_before + KB)
                            else:
                                sp.wait_ge(summed, batch_before * NC + KB * unit_before + 2 * h + 2)
                        if m == X_LOAD_AT and h == 0 and has(b, 1):
                            load_x(b, parity)
                        first = row * SB + h * 2 * P
                        sp.dma_start(in_pairs(w_ring[:, m % W_SLOTS, 2 * h:2 * h + 2, :]),
                                     node_pairs(adj[bass.ds(b, 1), first:first + 2 * P, col * SB:(col + 1) * SB]))\
                            .then_inc(w_landed[m % W_SLOTS][h], 16)
                if not has(b, 1):
                    load_x(b, parity)

            all_steps(sp, step)
            sp.wait_ge(out_stored, 16 * (B - 1))
            sp.wait_ge(end_stored, 16 * 4)

        @block.gpsimd
        def _(pool):
            pool.memset(ident[:, :], 0.0).then_inc(ident_zero, 1)
            pool.wait_ge(ident_zero, 1)
            pool.affine_select(out=ident[:, :], in_=ident[:, :], compare_op=ALU.not_equal, fill=1.0, base=0,
                               pattern=[[-1, P]], channel_multiplier=1).then_inc(ident_ready, 1)
            pool.wait_ge(ident_ready, 1)
            pool.tensor_copy(ident_bf16, ident[:, :]).then_inc(ident_ready, 1)

            def residual(q, parity):
                pool.wait_ge(y_scaled, 2 * q + 2)
                pool.tensor_tensor(res[:, :, :], res[:, :, :], x_in[parity][:, :, :], ALU.add).then_inc(x_added, 1)

            def by_row(values):
                return values[:, :].rearrange("p (t o) -> p t o", o=1).broadcast_to([P, NT, C])

            def centre(q):
                pool.wait_ge(mean_ready, q + 1)
                pool.tensor_tensor(res[:, :, :], res[:, :, :], by_row(neg_mean), ALU.add).then_inc(centred, 1)
                pool.wait_ge(centred, q + 1)
                pool.wait_ge(y_turned, 2 * q + 2)
                pool.tensor_tensor(square_of, res[:, :, :], res[:, :, :], ALU.mult).then_inc(squared, 1)

            def normalise(q):
                pool.wait_ge(rstd_ready, q + 1)
                pool.tensor_tensor(res[:, :, :], res[:, :, :], by_row(rstd), ALU.mult).then_inc(normed, 1)

            def step(b, parity):
                q = b - 2
                if not has(b, 0):
                    if has(b, 1):
                        residual(q, parity)
                        centre(q)
                        normalise(q)
                    return
                if due(count := b):
                    pool.wait_ge(col_summed, count)
                done = 0
                for c, (_, I, J, k, _, _) in enumerate(CHUNKS):
                    if has(b, 2):
                        if c == RESIDUAL_AT + 1:
                            residual(q, parity)
                        if c == CENTRE_AT + 1:
                            centre(q)
                        if c == NORMALISE_AT + 1:
                            normalise(q)
                    part = col_part(parity, c)
                    if part is None or (k == 0 and FIRST_UNIT[J] == (I, J)):
                        continue
                    if c in PE_SUMS and not has(b, 1):
                        continue
                    (first, width), chunk = part
                    acc = colacc[:, J * SB + first:J * SB + SB]
                    pool.wait_ge(s_ready, b * NC + c + 1)
                    if k == 1 and FIRST_UNIT[J] == (I, J):
                        (first0, width0), chunk0 = col_part(parity, c - 1)
                        pool.tensor_tensor(acc, chunk0[:, width0 - width:width0], chunk, ALU.add)\
                            .then_inc(cols_added, 1)
                        if first0 < first:
                            pool.tensor_copy(colacc[:, J * SB + first0:J * SB + first], chunk0[:, 0:width0 - width])\
                                .then_inc(cols_added, 1)
                            done += 1
                    else:
                        if due(count := cols_count(b, done)):
                            pool.wait_ge(cols_added, count)
                        pool.tensor_tensor(acc, acc, chunk, ALU.add).then_inc(cols_added, 1)
                    done += 1
                assert done == (NCOL if has(b, 1) else NCOL - len(PE_SUMS))

            all_steps(pool, step)

        @block.vector
        def _(dve):
            dve.memset(row_sums[:, :, :], 0.0).then_inc(consts_ready, 1)
            dve.memset(ones[:, :], 1.0).then_inc(consts_ready, 1)
            dve.memset(colacc[:, 0:P], 0.0).then_inc(consts_ready, 1)
            twice = u_left_side.rearrange("p t (two part) r -> p t two part r", two=2)
            for part in range(PARTS):
                if part == 0:
                    dve.wait_ge(u_landed, 16)
                else:
                    dve.wait_ge(rest_ready, part)
                dve.tensor_copy(twice[:, :, :, part, :], times(u_left[part], 2)).then_inc(left_ready, 1)
                if part + 1 < PARTS:
                    dve.wait_ge(left_ready, part + 1)
                    dve.tensor_tensor(u_left[part + 1], u_left[part], twice[:, :, 0, part, :], ALU.subtract)\
                        .then_inc(rest_ready, 1)
            dve.wait_ge(u_turned, 1)
            for i in range(2):
                dve.tensor_copy(half_of_u(u_t_left, i, 2 * PARTS), turned_u(y, i, 2 * PARTS)).then_inc(u_t_ready, 1)
            dve.wait_ge(u_turned, 2)
            dve.tensor_copy(half_of_u(u_t_right, 1, 2 * PARTS), turned_u(turned, 1, 2 * PARTS)).then_inc(u_t_ready, 1)
            dve.wait_ge(u_turned, 3)
            dve.tensor_copy(half_of_u(u_t_low, 1, PARTS), turned_u(mirror, 3, PARTS)).then_inc(u_t_ready, 1)
            dve.wait_ge(consts_ready, 3)
            dve.wait_ge(scale_landed, 16)

            def add_mirror(b, c):
                _, I, J, k, col0, width = CHUNKS[c]
                m = LOAD_OF[I, J]
                dve.wait_ge(mirrored, b * NC + c + 1)
                if k % 2 == 0:
                    dve.wait_ge(w_landed[m % W_SLOTS][k // 2], 16 * (b * (NL // W_SLOTS) + m // W_SLOTS + 1))
                first = col0 // P
                if first % 2 == 1:
                    bank = mirror[:, mirror_bank(c), 0:P]
                    last = dve.tensor_tensor(bank, bank, w_pairs(m, k, first, first + 1), ALU.add)
                    first += 1
                if first < KB:
                    bank = mirror[:, mirror_bank(c), P * first - col0:width]\
                        .rearrange("p (h two q) -> p h two q", two=2, q=P)
                    last = dve.tensor_tensor(bank, bank, w_pairs(m, k, first, KB), ALU.add)
                last.then_inc(summed, 1)

            def times_a(b, parity, c):
                u, I, J, k, col0, width = CHUNKS[c]
                dve.wait_ge(summed, b * NC + c + 1)
                if isinstance(b, int) and b == 0:
                    dve.wait_ge(a_ready, c + 1)
                if k == 0:
                    if u >= DOUBLED:
                        if due(count := (b - 1) * NB + UNIT_DONE[I, J]):
                            dve.wait_ge(back_used, count)
                    elif u == 0:
                        if due(count := (b - 1) * NB):
                            dve.wait_ge(back_used, count)
                at, a0 = S_AT[parity, I, J, k], A_AT[I, J, k]
                dve.scalar_tensor_tensor(out=s_store[:, at:at + width], in0=mirror[:, mirror_bank(c), 0:width],
                                         scalar=1.0, in1=a_store[:, a0:a0 + width], op0=ALU.mult, op1=ALU.mult,
                                         accum_out=row_sums[:, KB * I + k, J:J + 1]).then_inc(s_ready, 1)

            def degrees(p):
                dve.wait_ge(s_ready, (p + 1) * NC)
                dve.tensor_reduce(out=row_sum[:, :], in_=row_sums[:, :, :], axis=AX.X, op=ALU.add)\
                    .then_inc(row_summed, 1)
                dve.wait_ge(row_summed, p + 1)
                dve.wait_ge(deg_turned, p + 1)
                by_node = mirror[:, DEG_BANK, :].rearrange("p (k j q) -> p j k q", k=KB, j=KB)[:, :, :, 0]
                dve.tensor_tensor(deg[:, :].rearrange("p (j k) -> p j k", j=KB), by_node,
                                  row_sum[:, :].rearrange("p (j k) -> p j k", j=KB), ALU.add).then_inc(deg_added, 1)
                dve.wait_ge(deg_added, p + 1)
                dve.tensor_scalar(deg_half[:, :], deg[:, :], 0.5, DEG_EPS, ALU.mult, ALU.max).then_inc(deg_bounded, 1)
                dve.wait_ge(deg_bounded, p + 1)
                dve.reciprocal(deg_inv[:, :], deg_half[:, :]).then_inc(inv_ready, 1)

            def scale_x(p, parity):
                dve.wait_ge(d_ready, p + 1)
                dve.tensor_scalar(d_half[:, :], d[:, :], 0.5, None, ALU.mult).then_inc(d_halved, 1)
                dve.wait_ge(d_halved, p + 1)
                dve.wait_ge(x_landed[parity], x_count(p, parity))
                if due(count := p * NB):
                    dve.wait_ge(back_used, count)
                for odd in range(2):
                    dve.tensor_tensor(half_rows(x_scaled[:, :, :], odd), half_rows(x_in[parity][:, :, :], odd),
                                      half(d_half, odd).rearrange("p l (k o) -> p l k o", o=1)
                                      .broadcast_to([P, 2, KB, C]), ALU.mult).then_inc(x_ready, 1)
                dve.tensor_scalar(d_scale[parity][:, :], d[:, :], w_col[:, 0:1], None, ALU.mult).then_inc(d_scaled, 1)

            def scale_y(q, parity, bank):
                dve.wait_ge(y_turned, 2 * q + bank + 1)
                if bank == 0:
                    if due(count := 16 * q):
                        dve.wait_ge(out_stored, count)
                    dve.wait_ge(d_scaled, q + 1)
                scale = d_scale[parity][:, :].rearrange("p (l s k o) -> p l s k o", l=2, s=2, o=1)[:, :, bank]
                dve.tensor_tensor(
                    res[:, :, :].rearrange("p (l s k) c -> p l s k c", l=2, s=2)[:, :, bank],
                    mirror[:, Y_BANK[bank], :].rearrange("p (k l c) -> p l k c", k=KB, l=2),
                    scale.broadcast_to([P, 2, KB, C]), ALU.mult).then_inc(y_scaled, 1)

            def mean(q):
                dve.wait_ge(x_added, q + 1)
                dve.tensor_reduce(out=sums[:, :], in_=res[:, :, :], axis=AX.X, op=ALU.add).then_inc(row_added, 1)
                dve.wait_ge(row_added, q + 1)
                dve.tensor_scalar(neg_mean[:, :], sums[:, :], -1.0 / C, None, ALU.mult).then_inc(mean_ready, 1)

            def variance(q):
                dve.wait_ge(squared, q + 1)
                dve.tensor_reduce(out=squares[:, :], in_=square_of, axis=AX.X, op=ALU.add).then_inc(squares_summed, 1)
                dve.wait_ge(squares_summed, q + 1)
                dve.tensor_scalar(var[:, :], squares[:, :], 1.0 / C, LN_EPS, ALU.mult, ALU.add).then_inc(var_added, 1)
                dve.wait_ge(var_added, q + 1)
                dve.reciprocal(var_inv[:, :], var[:, :]).then_inc(var_ready, 1)

            def finish(q, parity, bank):
                def by_row(values):
                    return half(values, bank).rearrange("p l (k o) -> p l k o", o=1).broadcast_to([P, 2, KB, C])

                rows = half_rows(end_res, bank)
                dve.wait_ge(y_turned, 2 * q + bank + 1)
                dve.tensor_tensor(rows, mirror[:, Y_BANK[bank], :].rearrange("p (k l c) -> p l k c", k=KB, l=2),
                                  by_row(d_scale[parity]), ALU.mult).then_inc(end_scaled, 1)
                dve.wait_ge(end_scaled, bank + 1)
                dve.tensor_tensor(rows, rows, half_rows(x_in[parity][:, :, :], bank), ALU.add).then_inc(end_added, 1)
                dve.wait_ge(end_added, bank + 1)
                dve.tensor_reduce(out=half(sums, bank), in_=rows, axis=AX.X, op=ALU.add).then_inc(end_summed, 1)
                dve.wait_ge(end_summed, bank + 1)
                dve.tensor_scalar(half(neg_mean, bank), half(sums, bank), -1.0 / C, None, ALU.mult)\
                    .then_inc(end_mean, 1)
                dve.wait_ge(end_mean, bank + 1)
                dve.tensor_tensor(rows, rows, by_row(neg_mean), ALU.add).then_inc(end_centred, 1)
                dve.wait_ge(end_squared, bank + 1)
                dve.tensor_reduce(out=half(squares, bank), in_=half_rows(end_square, bank), axis=AX.X, op=ALU.add)\
                    .then_inc(end_squares, 1)
                dve.wait_ge(end_squares, bank + 1)
                dve.tensor_scalar(half(var, bank), half(squares, bank), 1.0 / C, LN_EPS, ALU.mult, ALU.add)\
                    .then_inc(end_var, 1)
                dve.wait_ge(end_var, bank + 1)
                dve.reciprocal(half(var_inv, bank), half(var, bank)).then_inc(end_inv, 1)
                dve.wait_ge(end_root, bank + 1)
                dve.tensor_tensor(rows, rows, by_row(rstd), ALU.mult).then_inc(end_normed, 1)

            def step(b, parity):
                p, q = b - 1, b - 2
                if not has(b, 1) and has(b, 2):
                    finish(q, parity, 1)
                    return
                if has(b, 1):
                    scale_x(p, 1 - parity)
                if has(b, 0):
                    add_mirror(b, 0)
                for c in range(NC):
                    if has(b, 0):
                        if c + 1 < NC:
                            add_mirror(b, c + 1)
                        times_a(b, parity, c)
                    if c == SCALE_Y_AT and has(b, 2):
                        scale_y(q, parity, 0)
                        scale_y(q, parity, 1)
                    if c == MEAN_AT and has(b, 2):
                        mean(q)
                    if c == VARIANCE_AT and has(b, 2):
                        variance(q)
                if has(b, 0):
                    degrees(b)
                elif has(b, 1):
                    dve.wait_ge(d_scaled, p + 1)
                    dve.wait_ge(rstd_ready, q + 1)
                    dve.wait_ge(normed, q + 1)
                    finish(p, 1 - parity, 0)

            all_steps(dve, step)

        @block.scalar
        def _(act):
            act.dma_start(w_col[:, :], w_scale.partition_broadcast(P)).then_inc(scale_landed, 16)
            act.wait_ge(scale_landed, 16)
            act.activation(rstd[:, 0:1], w_col[:, :], ACT.Sigmoid).then_inc(table_loaded, 1)
            for part in range(PARTS):
                if part == 0:
                    act.wait_ge(u_landed, 16)
                else:
                    act.wait_ge(rest_ready, part)
                target = u_right_low if part == PARTS - 1 else u_right_side[:, :, PARTS * part:PARTS * part + PARTS, :]
                act.activation(target, times(u_left[part], PARTS), ACT.Copy).then_inc(right_ready, 1)
            act.wait_ge(u_turned, 2)
            act.activation(half_of_u(u_t_right, 0, 2 * PARTS), turned_u(turned, 0, 2 * PARTS), ACT.Copy)\
                .then_inc(u_t_ready, 1)
            act.wait_ge(u_turned, 3)
            act.activation(half_of_u(u_t_low, 0, PARTS), turned_u(mirror, 2, PARTS), ACT.Copy).then_inc(u_t_ready, 1)
            act.wait_ge(table_loaded, 1)
            for c, (_, I, J, k, _, width) in enumerate(CHUNKS):
                act.wait_ge(a_logits, c + 1)
                a0 = A_AT[I, J, k]
                act.activation(a_store[:, a0:a0 + width], logit_bank(c)[:, 0:width], ACT.Sigmoid)\
                    .then_inc(a_ready, 1)

            def copy_y(q, bank, done):
                if bank == 0:
                    if due(count := 2 * q):
                        act.wait_ge(y_turned, count)
                    if due(count := q):
                        act.wait_ge(squares_summed, count)
                    if has(q, -1):
                        act.wait_ge(deg_turned, q + 2)
                act.wait_ge(back_used, q * NB + done)
                act.activation(y_t[:, bank, :], y[:, bank, :], ACT.Copy).then_inc(y_copied, 1)

            def copy_column_sums(p):
                if due(count := p - 1):
                    act.wait_ge(squares_summed, count)
                act.wait_ge(col_summed, p + 1)
                act.activation(col_sums, mirror[:, COL_BANK, :], ACT.Copy).then_inc(col_copied, 1)

            def root_degrees(p):
                act.wait_ge(inv_ready, p + 1)
                act.activation(d[:, :], deg_inv[:, :], ACT.Sqrt).then_inc(d_ready, 1)

            def copy_back(p, n, blocks):
                act.wait_ge(s_turned, p * NB + n + 1)
                if due(count := p * NB + n + 1 - BACK_SLOTS):
                    act.wait_ge(back_used, count)
                act.activation(back[:, n % BACK_SLOTS, 0:P * blocks], turned[:, n % BACK_BANKS, 0:P * blocks],
                               ACT.Copy).then_inc(back_ready, 1)

            def root_variance(q):
                act.wait_ge(var_ready, q + 1)
                act.activation(rstd[:, :], var_inv[:, :], ACT.Sqrt).then_inc(rstd_ready, 1)

            def store(q):
                act.wait_ge(normed, q + 1)
                act.dma_start(node_pairs(out[bass.ds(q, 1), :, :]), in_pairs(res[:, :, :]))\
                    .then_inc(out_stored, 16)

            def end_squares_of(bank):
                act.wait_ge(end_centred, bank + 1)
                act.activation(half_rows(end_square, bank), half_rows(end_res, bank), ACT.Square)\
                    .then_inc(end_squared, 1)

            def end_root_of(bank):
                act.wait_ge(end_inv, bank + 1)
                act.activation(half(rstd, bank), half(var_inv, bank), ACT.Sqrt).then_inc(end_root, 1)

            def end_store(q, bank):
                act.wait_ge(end_normed, bank + 1)
                for l in range(2):
                    first = KB * (2 * l + bank)
                    act.dma_start(node_pairs(out[bass.ds(q, 1), first * P:(first + KB) * P, :]),
                                  in_pairs(end_res[:, first:first + KB, :])).then_inc(end_stored, 16)

            def step(b, parity):
                p, q = b - 1, b - 2
                if not has(b, 1) and has(b, 2):
                    copy_y(q, 1, NB)
                    end_squares_of(1)
                    end_root_of(1)
                    end_store(q, 1)
                    act.wait_ge(end_stored, 16 * 4)
                    return
                if has(b, 2):
                    copy_y(q, 0, NB)
                for _, back_products in GROUPS if has(b, 0) else END_GROUPS:
                    for _, _, _, blocks, n in back_products:
                        if n == COPY_SUMS_AT and has(b, 0):
                            copy_column_sums(b)
                        if has(b, 1):
                            copy_back(p, n, blocks)
                        if n == COPY_Y_AT and has(b, 2):
                            copy_y(q, 1, NB)
                        if n == ROOT_AT and has(b, 2):
                            root_variance(q)
                        if n == (STORE_AT if has(b, 0) else END_STORE_AT) and has(b, 2):
                            store(q)
                        if not has(b, 0):
                            if n == END_COPY_AT:
                                copy_y(p, 0, END_HALF_DONE)
                            if n == END_SQUARE_AT:
                                end_squares_of(0)
                            if n == END_ROOT_AT:
                                end_root_of(0)
                            if n == END_HALF_STORE_AT:
                                end_store(p, 0)
                if has(b, 0):
                    root_degrees(b)

            all_steps(act, step)

        @block.tensor
        def _(pe):
            def turn_u():
                pe.wait_ge(ident_ready, 2)
                for parts, banks, bank0, parts_ready, count in (
                        (u_left_side, y, 0, left_ready, PARTS), (u_right_side, turned, 0, right_ready, PARTS - 1),
                        (u_right_low, mirror, 2, right_ready, PARTS)):
                    pe.wait_ge(parts_ready, count)
                    groups = 2 * PARTS if bank0 == 0 else PARTS
                    for t in range(NT):
                        last = pe.transpose(turned_u(banks, bank0 + t // (NT // 2), groups)[:, P * (t % (NT // 2)):P * (t % (NT // 2)) + P],
                                            parts[:, t, :, :].rearrange("p g r -> p (g r)"), ident_bf16)
                    last.then_inc(u_turned, 1)

            def logits(c):
                _, I, J, k, col0, width = CHUNKS[c]
                if c >= 4:
                    pe.wait_ge(a_ready, c - 3)
                rows, columns = slice(I * SB + k * P, I * SB + k * P + P), slice(J * SB + col0, J * SB + SB)
                out = logit_bank(c)[:, 0:width]
                pe.matmul(out, u_t_left[0:2 * PARTS * R, rows], u_t_right[0:2 * PARTS * R, columns],
                          start=True, stop=False)
                pe.matmul(out, u_t_left[0:PARTS * R, rows], u_t_low[0:PARTS * R, columns],
                          start=False, stop=True).then_inc(a_logits, 1)

            def turn_mirror(b, c):
                _, I, J, k, col0, _ = CHUNKS[c]
                m = LOAD_OF[J, I]
                what, n, step_before = ring_before("chunk", c)
                if what == "y":
                    if has(b, 2):
                        pe.wait_ge(y_scaled, 2 * (b - 2) + n + 1)
                elif what == "chunk":
                    if due(count := (b - step_before) * NC + n + 1):
                        pe.wait_ge(s_ready, count)
                elif what == "column sums":
                    if due(count := b):
                        pe.wait_ge(col_copied, count)
                elif due(count := b):
                    pe.wait_ge(deg_added, count)
                for j in range(col0 // P, KB):
                    if k == 0 and j % 2 == 0:
                        pe.wait_ge(w_landed[m % W_SLOTS][j // 2], 16 * (b * (NL // W_SLOTS) + m // W_SLOTS + 1))
                    last = pe.transpose(mirror[:, mirror_bank(c), P * j - col0:P * j - col0 + P],
                                        w_pairs(m, j, k, k + 1), ident[:, :])
                last.then_inc(mirrored, 1)

            def sum_columns(p):
                direct = [] if has(p, 1) else PE_SUMS
                pe.wait_ge(cols_added, cols_count(p, NCOL - len(direct)))
                pe.wait_ge(s_ready, (p + 1) * NC - len(direct))
                for J in range(KB):
                    last = pe.matmul(mirror[32 * J:32 * J + 32, COL_BANK, :], ones[:, :], colacc[:, J * SB:J * SB + SB],
                                     start=True, stop=not any(CHUNKS[c][2] == J for c in direct))
                for c in direct:
                    pe.wait_ge(s_ready, p * NC + c + 1)
                    _, I, J, k, _, _ = CHUNKS[c]
                    at = S_AT[0, I, J, k]
                    last = pe.matmul(mirror[32 * J:32 * J + 32, COL_BANK, :], ones[:, :], s_store[:, at:at + SB],
                                     start=False, stop=c == direct[-1])
                last.then_inc(col_summed, 1)

            def turn_column_sums(p):
                pe.wait_ge(col_copied, p + 1)
                for k in range(KB):
                    last = pe.transpose(mirror[:, DEG_BANK, P * k:P * k + P], col_sums[:, P * k:P * k + P], ident[:, :])
                last.then_inc(deg_turned, 1)

            def turn_y(q, bank):
                pe.wait_ge(y_copied, 2 * q + bank + 1)
                if has(q, -2):
                    pe.wait_ge(s_ready, (q + 2) * NC + ring_before("y", bank)[1] + 1)
                for k in range(KB):
                    last = pe.transpose(mirror[:, Y_BANK[bank], P * k:P * k + P], y_t[:, bank, P * k:P * k + P], ident[:, :])
                last.then_inc(y_turned, 1)

            def turn_back(p, parity, I, J, k, blocks, n):
                if due(count := p * NB + n + 1 - BACK_BANKS):
                    pe.wait_ge(back_ready, count)
                for i in range(blocks):
                    at = S_AT[parity, I, J, i] + P * (k - first_block(I, J, i))
                    last = pe.transpose(turned[:, n % BACK_BANKS, P * i:P * i + P], s_store[:, at:at + P], ident[:, :])
                last.then_inc(s_turned, 1)

            def group_turns(p, parity, g, groups):
                for I, J, k, blocks, n in groups[g][1]:
                    turn_back(p, parity, I, J, k, blocks, n)

            def group_products(p, parity, g, groups):
                natural, back_products = groups[g]
                first, last = ends_of_sums(groups)
                for I, J, k in natural:
                    at, block0 = S_AT[parity, I, J, k], first_block(I, J, k)
                    pe.matmul(y[lane(J), J % 2, P * block0:SB], x_scaled[:, KB * I + k, :],
                              s_store[:, at:at + SB - P * block0], start=first[J] == (g, "natural"),
                              stop=last[J] == (g, "natural"))
                for I, J, k, blocks, n in back_products:
                    pe.wait_ge(back_ready, p * NB + n + 1)
                    pe.matmul(y[lane(I), I % 2, 0:P * blocks], x_scaled[:, KB * J + k, :],
                              back[:, n % BACK_SLOTS, 0:P * blocks], start=first[I] == (g, "back"),
                              stop=last[I] == (g, "back")).then_inc(back_used, 1)

            def step(b, parity):
                p, q = b - 1, b - 2
                if not has(b, 1) and has(b, 0):
                    turn_u()
                if not has(b, 1) and has(b, 2):
                    turn_y(q, 1)
                    return
                order = tensor_order(has(b, 0), has(b, 1))
                groups = GROUPS if has(b, 0) else END_GROUPS
                odd_x, odd_y = first_odd(groups)
                for kind, n in order:
                    if kind == "mirror":
                        turn_mirror(b, n)
                        if has(b, 0) and not has(b, 1):
                            if n == 1:
                                pe.wait_ge(u_t_ready, 6)
                                logits(0)
                            if n == EARLY - 1:
                                for c in range(1, EARLY + 2):
                                    logits(c)
                            if EARLY <= n < NC - 2:
                                logits(n + 2)
                        if n == FIRST_TURNS_AT and has(b, 1):
                            group_turns(p, 1 - parity, 0, groups)
                    if kind == "group":
                        if n == 0:
                            if not has(b, 0):
                                group_turns(p, 1 - parity, 0, groups)
                        if n + 1 < len(groups):
                            group_turns(p, 1 - parity, n + 1, groups)
                        if n == 0:
                            pe.wait_ge(x_ready, 2 * p + 1)
                            if due(count := 2 * p - 1):
                                pe.wait_ge(y_copied, count)
                        if n == odd_x:
                            pe.wait_ge(x_ready, 2 * p + 2)
                        if n == odd_y:
                            if due(count := 2 * p):
                                pe.wait_ge(y_copied, count)
                        group_products(p, 1 - parity, n, groups)
                        if n in Y_TURN_AT and has(b, 2):
                            turn_y(q, Y_TURN_AT.index(n))
                        if n == END_HALF_GROUP + END_TURN_LAG and not has(b, 0):
                            turn_y(p, 0)
                    if has(b, 0):
                        if (kind, n) == (("group", SUM_AT) if has(b, 1) else order[-1]):
                            assert ("mirror", NC - 1) in order[:order.index((kind, n)) + 1]
                            sum_columns(b)
                        if (kind, n) == (("group", TURN_SUMS_AT) if has(b, 1) else order[-1]):
                            turn_column_sums(b)

            all_steps(pe, step)


_INS = ["x", "adj", "L0_gnn_U", "L0_gnn_w_scale"]


def kernel(**inputs):
    import numpy as _np
    import concourse.bacc as _bacc
    from concourse import mybir as _mybir
    from concourse.bass_utils import run_bass_kernel_spmd as _run

    nc = _bacc.Bacc("TRN2", target_bir_lowering=False, num_devices=1, dynamic_dma_scratch_size=1024)
    arrays, args = {}, []
    for name in _INS:
        a = _np.ascontiguousarray(inputs[name])
        if a.ndim == 0:
            a = a.reshape(1)
        arrays[f"in_{name}_dram"] = a
        args.append(nc.dram_tensor(f"in_{name}_dram", a.shape, _mybir.dt.from_np(a.dtype), kind="ExternalInput").ap())
    out = nc.dram_tensor("out_0_dram", (B, N, C), _mybir.dt.float32, kind="ExternalOutput").ap()
    propagate(nc, *args, out)
    r = _run(nc, [arrays], core_ids=[0])
    return r.results[0]["out_0_dram"]
```
